# Optimizing a Trainium2 kernel written in Bass

```python
import numpy as np
import jax
import jax.numpy as jnp

def _softmax(x, axis=-1):
    return jax.nn.softmax(x, axis=axis)

def _gelu(x):
    return jax.nn.gelu(x, approximate=True)

def _silu(x):
    return jax.nn.silu(x)

def _sigmoid(x):
    return jax.nn.sigmoid(x)

def _layernorm(x, axis=-1, eps=1e-05):
    m = jnp.mean(x, axis=axis, keepdims=True)
    v = jnp.var(x, axis=axis, keepdims=True)
    return (x - m) / jnp.sqrt(v + eps)

def _scatter_add(tgt, idx, src, axis=0):
    return tgt.at[idx].add(src)

def _segment_sum(src, seg, n):
    return jax.ops.segment_sum(src, seg, n)
kernel_name = 'mk_conv_preact_d4_conv_nchw64_r2_4673d9'

def setup_inputs(seed: int=0):
    np.random.seed(seed)
    _w = jnp.asarray

    def _rec_inputs():
        import jax
        import jax.numpy as jnp
        _gk = jax.random.key(seed)
        x = -0.000125 + 0.9999 * jax.random.normal(jax.random.fold_in(_gk, 1), (8, 32, 128, 128), jnp.float32)
        return x
    x = _rec_inputs()

    def _L0_conv_setup():
        import jax, jax.numpy as jnp
        import numpy as np
        from jax import lax
        BN_EPS = 1e-05
        SOBEL_X = np.array([[[[1, 0, -1], [2, 0, -2], [1, 0, -1]]]], dtype=np.float32)
        SOBEL_Y = np.array([[[[1, 2, 1], [0, 0, 0], [-1, -2, -1]]]], dtype=np.float32)

        def _forward(feature_map, conv_w, conv_b, bn_gamma, bn_beta, filt_x, filt_y):
            x = lax.conv_general_dilated(feature_map, conv_w, window_strides=(1, 1), padding=((1, 1), (1, 1)), dimension_numbers=('NCHW', 'OIHW', 'NCHW'))
            x = x + conv_b[None, :, None, None]
            mean = jnp.mean(x, axis=(0, 2, 3), keepdims=True)
            var = jnp.mean(jnp.square(x - mean), axis=(0, 2, 3), keepdims=True)
            x = (x - mean) * lax.rsqrt(var + BN_EPS)
            x = x * bn_gamma[None, :, None, None] + bn_beta[None, :, None, None]
            x = jax.nn.relu(x)
            B, C, H, W = x.shape
            Xf = jnp.fft.fft2(x, axes=(-2, -1))
            pad_h, pad_w = (H - filt_x.shape[-2], W - filt_x.shape[-1])
            fx = jnp.pad(filt_x, ((0, 0), (0, 0), (0, pad_h), (0, pad_w)))
            fy = jnp.pad(filt_y, ((0, 0), (0, 0), (0, pad_h), (0, pad_w)))
            Fx = jnp.fft.fft2(fx, axes=(-2, -1))
            Fy = jnp.fft.fft2(fy, axes=(-2, -1))
            grad_x = jnp.fft.ifft2(Xf * Fx, axes=(-2, -1)).real
            grad_y = jnp.fft.ifft2(Xf * Fy, axes=(-2, -1)).real
            second_xx = jnp.fft.ifft2(jnp.fft.fft2(grad_x, axes=(-2, -1)) * Fx, axes=(-2, -1)).real
            second_yy = jnp.fft.ifft2(jnp.fft.fft2(grad_y, axes=(-2, -1)) * Fy, axes=(-2, -1)).real
            curvature = second_xx + second_yy + jnp.square(grad_x) + jnp.square(grad_y) - 2.0 * grad_x * grad_y + x
            return curvature
        key = jax.random.key(seed)
        k1, k2, k3 = jax.random.split(key, 3)
        B, C_in, C_out, H, W = (8, 32, 32, 128, 128)
        feature_map = jax.random.normal(k1, (B, C_in, H, W), dtype=jnp.float32)
        conv_w = jax.random.normal(k2, (C_out, C_in, 3, 3), dtype=jnp.float32) * (1.0 / np.sqrt(C_in * 9))
        conv_b = jax.random.normal(k3, (C_out,), dtype=jnp.float32) * 0.01
        bn_gamma = jnp.ones((C_out,), dtype=jnp.float32)
        bn_beta = jnp.zeros((C_out,), dtype=jnp.float32)
        filt_x = jnp.asarray(SOBEL_X)
        filt_y = jnp.asarray(SOBEL_Y)
        return {'feature_map': feature_map, 'conv_w': conv_w, 'conv_b': conv_b, 'bn_gamma': bn_gamma, 'bn_beta': bn_beta, 'filt_x': filt_x, 'filt_y': filt_y}
    _L0_conv_all = _L0_conv_setup()
    _L0_conv_in = {k: v for k, v in _L0_conv_all.items() if k in ('conv_w', 'conv_b', 'bn_gamma', 'bn_beta', 'filt_x', 'filt_y')}
    del _L0_conv_all

    def _L1_conv_setup():
        import jax, jax.numpy as jnp
        import numpy as np
        K = 3
        K2 = K * K

        def _unfold(x):
            b, c, h, w = x.shape
            xp = jnp.pad(x, ((0, 0), (0, 0), (1, 1), (1, 1)))
            patches = jnp.stack([xp[:, :, i:i + h, j:j + w] for i in range(K) for j in range(K)], axis=2)
            return patches.transpose(0, 1, 3, 4, 2)
        key = jax.random.key(seed)
        k1, k2, k3, k4, k5 = jax.random.split(key, 5)
        b, c, h, w = (8, 32, 64, 64)
        out_c = 32
        x = jax.random.normal(k1, (b, c, h, w), dtype=jnp.float32)
        weight = jax.random.normal(k2, (c, out_c, K, K), dtype=jnp.float32) * 0.05
        bias = jax.random.normal(k3, (out_c,), dtype=jnp.float32) * 0.05
        op_w = jax.random.normal(k4, (K2 * K2, K2), dtype=jnp.float32) * 0.1
        op_b = jax.random.normal(k5, (K2 * K2,), dtype=jnp.float32) * 0.01
        return {'x': x, 'weight': weight, 'bias': bias, 'op_w': op_w, 'op_b': op_b}
    _L1_conv_all = _L1_conv_setup()
    _L1_conv_in = {k: v for k, v in _L1_conv_all.items() if k in ('weight', 'bias', 'op_w', 'op_b')}
    del _L1_conv_all

    def _L2_conv_setup():
        import jax, jax.numpy as jnp
        import numpy as np
        KSIZE = 5
        SIGMA1 = 1.0
        SIGMA2 = 2.0
        ALPHA = 1.0

        def _gaussian_kernel2d(ks, sigma):
            ax = jnp.arange(ks, dtype=jnp.float32) - (ks - 1) / 2.0
            xx, yy = jnp.meshgrid(ax, ax, indexing='ij')
            k = jnp.exp(-(xx ** 2 + yy ** 2) / (2.0 * sigma ** 2))
            return (k / k.sum()).reshape(1, 1, ks, ks)

        def _conv(x, k, pad):
            return jax.lax.conv_general_dilated(x, k, window_strides=(1, 1), padding=[(pad, pad), (pad, pad)], dimension_numbers=('NCHW', 'OIHW', 'NCHW'))
        key = jax.random.key(seed)
        kx, kw, kb = jax.random.split(key, 3)
        x = jax.random.normal(kx, (8, 32, 128, 128), dtype=jnp.float32)
        gate_w = jax.random.normal(kw, (1,), dtype=jnp.float32)
        gate_b = jax.random.normal(kb, (1,), dtype=jnp.float32)
        return {'x': x, 'gate_w': gate_w, 'gate_b': gate_b}
    _L2_conv_all = _L2_conv_setup()
    _L2_conv_in = {k: v for k, v in _L2_conv_all.items() if k in ('gate_w', 'gate_b')}
    del _L2_conv_all

    def _L3_conv_setup():
        import jax, jax.numpy as jnp
        import numpy as np
        B, IN_CH, OUT_CH, H, W = (16, 32, 32, 128, 128)
        MODES, KS = (16, 3)

        def _global_transform(c, w1, w2):
            m = MODES
            b, _, h, w = c.shape
            c_ft = jnp.fft.rfft2(c)
            top = jnp.einsum('bixy,ioxy->boxy', c_ft[:, :, :m, :m], w1)
            bot = jnp.einsum('bixy,ioxy->boxy', c_ft[:, :, -m:, :m], w2)
            out_ft = jnp.zeros((b, OUT_CH, h, w // 2 + 1), dtype=c_ft.dtype)
            out_ft = out_ft.at[:, :, :m, :m].set(top).at[:, :, -m:, :m].set(bot)
            return jnp.fft.irfft2(out_ft, s=(h, w))

        def _local_transform(c, conv_w, conv_b):
            pad = KS // 2
            xp = jnp.pad(c, ((0, 0), (0, 0), (pad, pad), (pad, pad)), mode='wrap')
            y = jax.lax.conv_general_dilated(xp, conv_w, window_strides=(1, 1), padding='VALID', dimension_numbers=('NCHW', 'OIHW', 'NCHW'))
            return y + conv_b[None, :, None, None]
        key = jax.random.key(seed)
        ks = jax.random.split(key, 8)
        scale = 1.0 / (IN_CH * OUT_CH)
        c = jax.random.normal(ks[0], (B, IN_CH, H, W), dtype=jnp.float32)
        w1r = scale * jax.random.uniform(ks[1], (IN_CH, OUT_CH, MODES, MODES), dtype=jnp.float32)
        w1i = scale * jax.random.uniform(ks[2], (IN_CH, OUT_CH, MODES, MODES), dtype=jnp.float32)
        w2r = scale * jax.random.uniform(ks[3], (IN_CH, OUT_CH, MODES, MODES), dtype=jnp.float32)
        w2i = scale * jax.random.uniform(ks[4], (IN_CH, OUT_CH, MODES, MODES), dtype=jnp.float32)
        fan_in = IN_CH * KS * KS
        bound = 1.0 / np.sqrt(fan_in)
        conv_w = jax.random.uniform(ks[5], (OUT_CH, IN_CH, KS, KS), minval=-bound, maxval=bound, dtype=jnp.float32)
        conv_b = jax.random.uniform(ks[6], (OUT_CH,), minval=-bound, maxval=bound, dtype=jnp.float32)
        return {'c': c, 'w1r': w1r, 'w1i': w1i, 'w2r': w2r, 'w2i': w2i, 'conv_w': conv_w, 'conv_b': conv_b}
    _L3_conv_all = _L3_conv_setup()
    _L3_conv_in = {k: v for k, v in _L3_conv_all.items() if k in ('w1r', 'w1i', 'w2r', 'w2i', 'conv_w', 'conv_b')}
    del _L3_conv_all
    return {'x': x, 'L0_conv_conv_w': _L0_conv_in['conv_w'], 'L0_conv_conv_b': _L0_conv_in['conv_b'], 'L0_conv_bn_gamma': _L0_conv_in['bn_gamma'], 'L0_conv_bn_beta': _L0_conv_in['bn_beta'], 'L0_conv_filt_x': _L0_conv_in['filt_x'], 'L0_conv_filt_y': _L0_conv_in['filt_y'], 'L1_conv_weight': _L1_conv_in['weight'], 'L1_conv_bias': _L1_conv_in['bias'], 'L1_conv_op_w': _L1_conv_in['op_w'], 'L1_conv_op_b': _L1_conv_in['op_b'], 'L2_conv_gate_w': _L2_conv_in['gate_w'], 'L2_conv_gate_b': _L2_conv_in['gate_b'], 'L3_conv_w1r': _L3_conv_in['w1r'], 'L3_conv_w1i': _L3_conv_in['w1i'], 'L3_conv_w2r': _L3_conv_in['w2r'], 'L3_conv_w2i': _L3_conv_in['w2i'], 'L3_conv_conv_w': _L3_conv_in['conv_w'], 'L3_conv_conv_b': _L3_conv_in['conv_b']}

def reference(x, L0_conv_conv_w, L0_conv_conv_b, L0_conv_bn_gamma, L0_conv_bn_beta, L0_conv_filt_x, L0_conv_filt_y, L1_conv_weight, L1_conv_bias, L1_conv_op_w, L1_conv_op_b, L2_conv_gate_w, L2_conv_gate_b, L3_conv_w1r, L3_conv_w1i, L3_conv_w2r, L3_conv_w2i, L3_conv_conv_w, L3_conv_conv_b):
    import jax
    import jax.numpy as jnp

    def _L0_conv_ref(feature_map, conv_w, conv_b, bn_gamma, bn_beta, filt_x, filt_y):
        import jax, jax.numpy as jnp
        import numpy as np
        from jax import lax
        BN_EPS = 1e-05
        SOBEL_X = np.array([[[[1, 0, -1], [2, 0, -2], [1, 0, -1]]]], dtype=np.float32)
        SOBEL_Y = np.array([[[[1, 2, 1], [0, 0, 0], [-1, -2, -1]]]], dtype=np.float32)

        def _forward(feature_map, conv_w, conv_b, bn_gamma, bn_beta, filt_x, filt_y):
            x = lax.conv_general_dilated(feature_map, conv_w, window_strides=(1, 1), padding=((1, 1), (1, 1)), dimension_numbers=('NCHW', 'OIHW', 'NCHW'))
            x = x + conv_b[None, :, None, None]
            mean = jnp.mean(x, axis=(0, 2, 3), keepdims=True)
            var = jnp.mean(jnp.square(x - mean), axis=(0, 2, 3), keepdims=True)
            x = (x - mean) * lax.rsqrt(var + BN_EPS)
            x = x * bn_gamma[None, :, None, None] + bn_beta[None, :, None, None]
            x = jax.nn.relu(x)
            B, C, H, W = x.shape
            Xf = jnp.fft.fft2(x, axes=(-2, -1))
            pad_h, pad_w = (H - filt_x.shape[-2], W - filt_x.shape[-1])
            fx = jnp.pad(filt_x, ((0, 0), (0, 0), (0, pad_h), (0, pad_w)))
            fy = jnp.pad(filt_y, ((0, 0), (0, 0), (0, pad_h), (0, pad_w)))
            Fx = jnp.fft.fft2(fx, axes=(-2, -1))
            Fy = jnp.fft.fft2(fy, axes=(-2, -1))
            grad_x = jnp.fft.ifft2(Xf * Fx, axes=(-2, -1)).real
            grad_y = jnp.fft.ifft2(Xf * Fy, axes=(-2, -1)).real
            second_xx = jnp.fft.ifft2(jnp.fft.fft2(grad_x, axes=(-2, -1)) * Fx, axes=(-2, -1)).real
            second_yy = jnp.fft.ifft2(jnp.fft.fft2(grad_y, axes=(-2, -1)) * Fy, axes=(-2, -1)).real
            curvature = second_xx + second_yy + jnp.square(grad_x) + jnp.square(grad_y) - 2.0 * grad_x * grad_y + x
            return curvature
        return _forward(feature_map, conv_w, conv_b, bn_gamma, bn_beta, filt_x, filt_y)

    def _L1_conv_ref(x, weight, bias, op_w, op_b):
        import jax, jax.numpy as jnp
        import numpy as np
        K = 3
        K2 = K * K

        def _unfold(x):
            b, c, h, w = x.shape
            xp = jnp.pad(x, ((0, 0), (0, 0), (1, 1), (1, 1)))
            patches = jnp.stack([xp[:, :, i:i + h, j:j + w] for i in range(K) for j in range(K)], axis=2)
            return patches.transpose(0, 1, 3, 4, 2)
        b, c, h, w = x.shape
        xu = _unfold(x)
        n = jnp.sqrt(jnp.sum(xu * xu, axis=1))
        op = jnp.tanh(n @ op_w.T + op_b).reshape(b, h, w, K2, K2)
        x_op = jnp.einsum('bchwj,bhwjk->bchwk', xu, op)
        wr = weight.reshape(c, -1, K2).transpose(1, 0, 2)
        out = jnp.einsum('bchwk,ock->bohw', x_op + xu, wr)
        return out + bias[None, :, None, None]

    def _L2_conv_ref(x, gate_w, gate_b):
        import jax, jax.numpy as jnp
        import numpy as np
        KSIZE = 5
        SIGMA1 = 1.0
        SIGMA2 = 2.0
        ALPHA = 1.0

        def _gaussian_kernel2d(ks, sigma):
            ax = jnp.arange(ks, dtype=jnp.float32) - (ks - 1) / 2.0
            xx, yy = jnp.meshgrid(ax, ax, indexing='ij')
            k = jnp.exp(-(xx ** 2 + yy ** 2) / (2.0 * sigma ** 2))
            return (k / k.sum()).reshape(1, 1, ks, ks)

        def _conv(x, k, pad):
            return jax.lax.conv_general_dilated(x, k, window_strides=(1, 1), padding=[(pad, pad), (pad, pad)], dimension_numbers=('NCHW', 'OIHW', 'NCHW'))
        gk1 = _gaussian_kernel2d(KSIZE, SIGMA1).astype(x.dtype)
        gk2 = _gaussian_kernel2d(KSIZE, SIGMA2).astype(x.dtype)
        sobel_x = jnp.array([[-1, 0, 1], [-2, 0, 2], [-1, 0, 1]], dtype=x.dtype).reshape(1, 1, 3, 3)
        sobel_y = jnp.array([[-1, -2, -1], [0, 0, 0], [1, 2, 1]], dtype=x.dtype).reshape(1, 1, 3, 3)
        x_gray = jnp.mean(x, axis=1, keepdims=True)
        pad = KSIZE // 2
        g1 = _conv(x_gray, gk1, pad)
        g2 = _conv(x_gray, gk2, pad)
        dog = g1 - g2
        gx = _conv(dog, sobel_x, 1)
        gy = _conv(dog, sobel_y, 1)
        mag = jnp.sqrt(gx * gx + gy * gy + 1e-06)
        att = jax.nn.sigmoid(mag * gate_w[0] + gate_b[0])
        return x * (1.0 + ALPHA * att)

    def _L3_conv_ref(c, w1r, w1i, w2r, w2i, conv_w, conv_b):
        import jax, jax.numpy as jnp
        import numpy as np
        B, IN_CH, OUT_CH, H, W = (16, 32, 32, 128, 128)
        MODES, KS = (16, 3)

        def _global_transform(c, w1, w2):
            m = MODES
            b, _, h, w = c.shape
            c_ft = jnp.fft.rfft2(c)
            top = jnp.einsum('bixy,ioxy->boxy', c_ft[:, :, :m, :m], w1)
            bot = jnp.einsum('bixy,ioxy->boxy', c_ft[:, :, -m:, :m], w2)
            out_ft = jnp.zeros((b, OUT_CH, h, w // 2 + 1), dtype=c_ft.dtype)
            out_ft = out_ft.at[:, :, :m, :m].set(top).at[:, :, -m:, :m].set(bot)
            return jnp.fft.irfft2(out_ft, s=(h, w))

        def _local_transform(c, conv_w, conv_b):
            pad = KS // 2
            xp = jnp.pad(c, ((0, 0), (0, 0), (pad, pad), (pad, pad)), mode='wrap')
            y = jax.lax.conv_general_dilated(xp, conv_w, window_strides=(1, 1), padding='VALID', dimension_numbers=('NCHW', 'OIHW', 'NCHW'))
            return y + conv_b[None, :, None, None]
        w1 = w1r + 1j * w1i
        w2 = w2r + 1j * w2i
        g = _global_transform(c, w1, w2)
        l = _local_transform(c, conv_w, conv_b)
        return g * l

    def _gn(v, G=32, eps=1e-05):
        B_, C_, H_, W_ = v.shape
        g = v.reshape(B_, G, C_ // G, H_, W_)
        m = jnp.mean(g, axis=(2, 3, 4), keepdims=True)
        s = jnp.var(g, axis=(2, 3, 4), keepdims=True)
        return ((g - m) / jnp.sqrt(s + eps)).reshape(v.shape)

    def _ln_c(v, eps=1e-06):
        m = jnp.mean(v, axis=1, keepdims=True)
        s = jnp.var(v, axis=1, keepdims=True)
        return (v - m) / jnp.sqrt(s + eps)

    def _ln_t(v, eps=1e-05):
        m = jnp.mean(v, axis=-1, keepdims=True)
        s = jnp.var(v, axis=-1, keepdims=True)
        return (v - m) / jnp.sqrt(s + eps)

    def _to_tokens(v):
        B_, C_, H_, W_ = v.shape
        return v.reshape(B_, C_, H_ * W_).transpose(0, 2, 1)

    def _from_tokens(t, like):
        B_, C_, H_, W_ = like.shape
        return t.transpose(0, 2, 1).reshape(B_, C_, H_, W_)
    x = x + _L0_conv_ref(_gn(x), L0_conv_conv_w, L0_conv_conv_b, L0_conv_bn_gamma, L0_conv_bn_beta, L0_conv_filt_x, L0_conv_filt_y)
    x = x + _L1_conv_ref(_gn(x), L1_conv_weight, L1_conv_bias, L1_conv_op_w, L1_conv_op_b)
    x = x + _L2_conv_ref(_gn(x), L2_conv_gate_w, L2_conv_gate_b)
    x = x + _L3_conv_ref(_gn(x), L3_conv_w1r, L3_conv_w1i, L3_conv_w2r, L3_conv_w2i, L3_conv_conv_w, L3_conv_conv_b)
    return x

_drawn_inputs = setup_inputs


def setup_inputs(seed=0):
    import zlib

    import numpy as np

    out = dict(_drawn_inputs(seed))
    spreads = {'L0_conv_bn_gamma': (1.0, 0.2), 'L0_conv_bn_beta': (0.0, 0.1)}
    factors = {'L0_conv_conv_b': 200.0,
     'L1_conv_bias': 31.181,
     'L1_conv_op_b': 64.0,
     'L3_conv_w1r': 64.0,
     'L3_conv_w1i': 64.0,
     'L3_conv_w2r': 193.612,
     'L3_conv_w2i': 193.002,
     'L3_conv_conv_w': 64.0,
     'L3_conv_conv_b': 200.0}
    for name, (base, spread) in spreads.items():
        noise = np.random.default_rng([zlib.crc32(name.encode()), seed]).standard_normal(out[name].shape)
        drawn = base * np.exp(spread * noise) if base else spread * noise
        out[name] = jnp.asarray(drawn.astype(out[name].dtype))
    for name, factor in factors.items():
        out[name] = (out[name] * factor).astype(out[name].dtype)
    return out
```

```python
from contextlib import ExitStack

import concourse.bass as bass
from concourse import mybir

F32 = mybir.dt.float32
BF16 = mybir.dt.bfloat16
ALU = mybir.AluOpType
ACT = mybir.ActivationFunctionType
AX = mybir.AxisListType

B, C, H, W = 8, 32, 128, 128
P = 128
G = P // C
RB = H // G
PW = W + 2
PLANE = (H + 2) * PW
TAIL = 8
CR = 4
CHUNKS = RB // CR
SPAN = CR * PW
NPX = CR * W
TAPS = 9
STACKS = 3
COMBOS = 21
ITEMS = 2 * COMBOS
MODES = 16
KX = 2 * MODES
BIAS_ROWS = 3
PAIRS = [(0, 0), (1, 0), (2, 0), (0, 1), (1, 1), (0, 2)]
KROWS = BIAS_ROWS + TAPS * len(PAIRS)
GN_EPS = BN_EPS = 1e-5
MAG_EPS = 1e-6
TRING = 6
START = 1
EVAC_CREDIT = 1
TANH_CREDIT = 2
MIX_CREDIT = 2
PAIR_ITEMS, PAIR_COMBOS = 2 * ITEMS, 2 * COMBOS
YPW = W + 4

CONST = {}
_at = 0
for _name, _n in (("mean", P), ("var", P), ("same_o", P), ("quarter", P), ("eye_o", C), ("shift", 5 * P), ("dog", 5 * P),
                  ("sobel", 5 * P), ("dft_h", 2 * KX), ("dft_w", 4 * MODES), ("idft_w", 2 * W), ("idft_h", 2 * H), ("parts", 3)):
    CONST[_name] = (_at, _at + _n)
    _at += _n
NCONST = _at


def pool_item(i):
    return i % 4 == 3


def tap_pair(s, q):
    if s < 18:
        return (4 * (s // 9) + q, s % 9)
    k = 4 * (s - 18) + q
    return (8, k) if k < TAPS else None


def stack_of(s):
    return s // 9 if s < 18 else 2


class Ticks:

    def __init__(self, eng, sem, base=0):
        self.eng, self.sem, self.base, self.n = eng, sem, base, 0

    def inc(self, ins):
        ins.then_inc(self.sem, 1)
        self.n += 1
        return ins

    def wait(self):
        self.eng.wait_ge(self.sem, START + self.base + self.n)


def four_layers(nc, x, conv0_w, conv0_b, bn_gamma, bn_beta, filt_x, filt_y, conv1_w, mix1_w, conv1_b, op_rows,
                gate_w, gate_b, w1r, w1i, w2r, w2i, conv3_w, conv3_b, consts, out):
    def dram(name, shape, dt=F32):
        return nc.dram_tensor(name, shape, dt, kind="Internal")

    pad_zero = dram("pad_zero", (C * PLANE + TAIL,))
    pad_wrap = dram("pad_wrap", (C * PLANE + TAIL,))
    norm_parts = dram("norm_parts", (3 * PLANE + TAIL,), BF16)
    ones_dram = dram("ones_dram", (BIAS_ROWS * H * PW,), BF16)
    y_dram = dram("y_dram", (B, C, H, W)).ap()
    l1_dram = dram("l1_dram", (C, H, W)).ap()
    l3_dram = dram("l3_dram", (B, C, H, W)).ap()
    x3_dram = dram("x3_dram", (B, C, H, W)).ap()
    spec_dram = dram("spec_dram", (KX, C, B * 2 * MODES)).ap()

    def plane_view(t, parts, dt_rows=H):
        return bass.AP(tensor=t, offset=0, ap=[[PW, H + 2], [PLANE, parts], [1, PW]])

    def tap_view(t):
        return bass.AP(tensor=t, offset=0, ap=[[PLANE, C], [RB * PW, G], [1, (RB - CR + 2) * PW + 2 + SPAN]])

    def flat(t, n, size):
        return bass.AP(tensor=t, offset=n, ap=[[size, 1], [1, size]])

    with ExitStack() as ctx:
        def sb(name, shape, dt=F32):
            return ctx.enter_context(nc.sbuf_tensor(name, shape, dt))

        def once(name):
            return ctx.enter_context(nc.semaphore(name))

        counted = []

        def sem(name):
            counted.append(once(name))
            return counted[-1]

        xh = sb("xh", [P, C, W])
        xn = sb("xn", [P, C, PW])
        tmp = sb("tmp", [P, C, W])
        norms = sb("norms", [P, (H * PW)], BF16)
        stack = sb("stack", [P, 2, STACKS, G, SPAN])
        ring = sb("ring", [P, TRING, 2 * NPX])
        lo = sb("lo", [P, 2, NPX])
        sq = sb("sq", [P, 2, NPX])
        k = sb("k", [P, NCONST])
        circ = sb("circ", [P, 8, P])
        opw = sb("opw", [KROWS, COMBOS, P], BF16)
        w_mix = sb("w_mix", [P, COMBOS, C])
        w_conv = sb("w_conv", [P, 3, STACKS, C])
        bias = sb("bias", [P, 3])
        st = sb("st", [P, C, 6])
        dev = sb("dev", [P, C, 2])
        dev2 = sb("dev2", [P, C, 2])
        mu = sb("mu", [P, C])
        sd = sb("sd", [P, C])
        rstd = sb("rstd", [P, C])
        eps = sb("eps", [P, 2])
        bst = sb("bst", [P, B * CHUNKS, 6])
        bagg = sb("bagg", [P, 2])
        bsm = sb("bsm", [P, 8])
        bexp = sb("bexp", [P, 2 * C])
        bn_a = sb("bn_a", [P, C])
        bn_b = sb("bn_b", [P, C])
        bn_m = sb("bn_m", [P, 2 * C])
        gam = sb("gam", [P, 2 * C])
        fil = sb("fil", [P, 2 * TAPS])
        f3 = sb("f3", [P, 9])
        f5 = sb("f5", [P, 5, 5])
        gate = sb("gate", [P, 2])
        r2 = sb("r2", [P, W])
        rn = sb("rn", [P, W])
        ra = sb("ra", [P, W])
        rp = sb("rp", [P, 3, PW], BF16)
        gray = sb("gray", [P, W + 4])
        dog = sb("dog", [P, W + 2])
        cs = sb("cs", [P, 3, 2, 4, MODES, B])
        ps = ctx.enter_context(nc.psum_tensor("ps", [P, 8, NPX], F32))

        normsf = norms[:, :].bitcast(F32)
        yp = normsf[:, 0:C * YPW].rearrange("p (c w) -> p c w", c=C)
        stackf = stack[:, :, :, :, :].rearrange("p a s g n -> p (a s g n)")
        op_in = stackf[0:KROWS, 0:COMBOS * P]
        op_rest = ring[:, :, :].rearrange("p a n -> p (a n)")[0:KROWS, 0:COMBOS * P]
        ones = norms[:, 0:BIAS_ROWS * H * PW // P]
        ringf = ring[:, :, :].rearrange("p a n -> p (a n)")
        z = ringf[:, 0:C * 2 * KX].rearrange("p (c r x) -> p c r x", c=C, r=2)
        wm = stackf[:, 0:4 * C * 64].rearrange("p (r t o m) -> p r t o m", r=2, t=2, o=C)
        ys = ringf[:, 0:2048].rearrange("p (a b m) -> p a b m", a=8, b=B)
        v2 = normsf[0:KX, 0:C * B * 2 * MODES].rearrange("p (o b m) -> p o b m", o=C, b=B)
        v2b = sq[0:KX, :, :].rearrange("p a n -> p (a n)").rearrange("p (o m) -> p o m", o=C)
        u = ringf[:, 2048:4096].rearrange("p (m n) -> p m n", m=8)

        def const(name, rows=P):
            a, b = CONST[name]
            return k[0:rows, a:b]

        shift = const("shift").rearrange("p (a n) -> p a n", a=5)
        dogm = const("dog").rearrange("p (a n) -> p a n", a=5)
        sobm = const("sobel").rearrange("p (a n) -> p a n", a=5)
        dftw = const("dft_w").rearrange("p (r n) -> p r n", r=2)
        idftw = const("idft_w").rearrange("p (s n) -> p s n", s=2)

        const_loaded, par_loaded, border_done = once("const_loaded"), once("par_loaded"), sem("border_done")
        init_done, op_ready, filt_ready = once("init_done"), once("op_ready"), once("filt_ready")
        x_loaded, y_loaded, branch_loaded = sem("x_loaded"), sem("y_loaded"), sem("branch_loaded")
        step = sem("step")
        act_step = sem("act_step")
        gn_stats, gn_mean, gn_dev, gn_var, gn_sd, gn_out = (sem(n) for n in ("gn_stats", "gn_mean", "gn_dev", "gn_var", "gn_sd", "gn_out"))
        xn_stored, stack_loaded = sem("xn_stored"), [sem("stack_loaded0"), sem("stack_loaded1")]
        chunk_mm, chunk_evac, chunk_stat = sem("chunk_mm"), sem("chunk_evac"), sem("chunk_stat")
        lo_stored = [sem("lo_stored0"), sem("lo_stored1")]
        bn_dev, bn_mat, bn_sd, bn_ready, bn_act = (once(n) for n in ("bn_dev", "bn_mat", "bn_sd", "bn_ready", "bn_act"))
        bn_applied, relu_done, filt_mm, filt_sq, filt_used = (sem(n) for n in ("bn_applied", "relu_done", "filt_mm", "filt_sq", "filt_used"))
        norm_sq, norm_sum, norm_root, norm_split, parts_stored, norms_loaded = (sem(n) for n in (
            "norm_sq", "norm_sum", "norm_root", "norm_split", "parts_stored", "norms_loaded"))
        spread_mm, tanh_done, prod_dve, prod_pool, mix_mm = (sem(n) for n in ("spread_mm", "tanh_done", "prod_dve", "prod_pool", "mix_mm"))
        gray_done, dog_mm, dog_copy, sob_mm, sob_sq, mag_sum, att_act, att_mul, x3_done, x3_stored = (sem(n) for n in (
            "gray_done", "dog_mm", "dog_copy", "sob_mm", "sob_sq", "mag_sum", "att_act", "att_mul", "x3_done", "x3_stored"))
        dfth_mm, dfth_copy, dftw_mm, dftw_copy = (sem(n) for n in ("dfth_mm", "dfth_copy", "dftw_mm", "dftw_copy"))
        wm_loaded, spec_mm, spec_copy, spec_stored, spec_loaded = (once(n) for n in ("wm_loaded", "spec_mm", "spec_copy", "spec_stored", "spec_loaded"))
        slice_done, idfth_mm, idfth_copy, idftw_mm, out_mul, out_done, out_stored = (sem(n) for n in (
            "slice_done", "idfth_mm", "idfth_copy", "idftw_mm", "out_mul", "out_done", "out_stored"))

        def settle(eng):
            eng.nop(nofuse=True)

        block = ctx.enter_context(nc.Block())

        NCONV_DMA, NMIX_DMA = TAPS, 4 * STACKS
        HALF = CHUNKS // 2
        LOAD1, LOADM, LOAD3 = 16 * NCONV_DMA * HALF, 16 * NMIX_DMA * HALF, 16 * NCONV_DMA * HALF
        PARS = 14
        BORDERS = 12
        LEAD = 2
        pool_items = sum(pool_item(n) for n in range(PAIR_ITEMS))
        dve_items = PAIR_ITEMS - pool_items

        @block.sync
        def _(sp):
            def load_stacks(src, chunk_rows, par, whole):
                view = tap_view(src)
                for j in range(4 * STACKS if whole else TAPS):
                    s, q = divmod(j, 4)
                    dy, dx = divmod(min(j, 8), 3)
                    sp.dma_start(stack[C * q:C * q + C, par, s, :, :],
                                 view[:, :, bass.ds(chunk_rows * PW + dy * PW + dx, SPAN)]).then_inc(stack_loaded[par], 16)

            def load_rows(tile, image, loaded):
                for h0 in (0, H // 2):
                    sp.dma_start(tile[h0:h0 + H // 2, :, :], image.rearrange("c h w -> h c w")[h0:h0 + H // 2]).then_inc(loaded, 16)

            def conv_stacks(src, conv0):
                sp.wait_ge(chunk_mm, START + conv0)
                for par in range(2):
                    load_stacks(src, par * CR, par, False)
                with sp.Fori(1, HALF) as i:
                    for par in range(2):
                        sp.wait_ge(chunk_mm, START + conv0 + 2 * i - (1 - par))
                        load_stacks(src, (2 * i + par) * CR, par, False)

            sp.dma_start(k[:, :], consts).then_inc(const_loaded, 16)
            for dst, src in ((op_in, op_rows), (w_mix[:, :, :], mix1_w), (w_conv[:, 0, :, :], conv0_w), (w_conv[:, 1, :, :], conv1_w),
                             (w_conv[:, 2, :, :], conv3_w), (bias[:, 0:1], conv0_b), (bias[:, 1:2], conv1_b), (bias[:, 2:3], conv3_b),
                             (gam[:, 0:C], bn_gamma.partition_broadcast(P)), (gam[:, C:2 * C], bn_beta.partition_broadcast(P)),
                             (fil[:, 0:TAPS], filt_x.partition_broadcast(P)), (fil[:, TAPS:], filt_y.partition_broadcast(P)),
                             (gate[:, 0:1], gate_w.partition_broadcast(P))):
                sp.dma_start(dst, src).then_inc(par_loaded, 16)
            sp.dma_start(gate[:, 1:2], gate_b.partition_broadcast(P)).then_inc(par_loaded, 16)
            sp.wait_ge(init_done, 1)
            zero_rows = tmp[0:C, 0, :]
            for row in (0, H + 1):
                for c0, n in ((0, W), (W, PW - W)):
                    sp.dma_start(plane_view(pad_zero, C)[row, :, c0:c0 + n], zero_rows[:, 0:n]).then_inc(border_done, 16)
                    sp.dma_start(plane_view(norm_parts, 3)[row, :, c0:c0 + n], rp[0:3, 0, 0:n]).then_inc(border_done, 16)
            sp.dma_start(flat(pad_zero, C * PLANE, TAIL), tmp[0:1, 0, 0:TAIL]).then_inc(border_done, 16)
            sp.dma_start(flat(pad_wrap, C * PLANE, TAIL), tmp[0:1, 0, 0:TAIL]).then_inc(border_done, 16)
            sp.dma_start(flat(norm_parts, 3 * PLANE, TAIL), rp[0:1, 0, 0:TAIL]).then_inc(border_done, 16)
            sp.dma_start(bass.AP(tensor=ones_dram, offset=0, ap=[[BIAS_ROWS * H * PW // P, P], [1, BIAS_ROWS * H * PW // P]]),
                         ones[:, :]).then_inc(border_done, 16)
            sp.wait_ge(border_done, START + 16 * BORDERS)
            sp.wait_ge(op_ready, 1)

            with sp.Fori(0, B) as b:
                sp.wait_ge(gn_out, START + b)
                load_rows(xh, x[b], x_loaded)
                sp.wait_ge(gn_out, START + b + 1)
                sp.dma_start(plane_view(pad_zero, C)[1:H + 1], xn[:, :, :]).then_inc(xn_stored, 16)
                sp.wait_ge(xn_stored, START + 16 * (b + 1))
                settle(sp)
                conv_stacks(pad_zero, b * CHUNKS)
                for par in range(2):
                    sp.wait_ge(stack_loaded[par], START + LOAD1 * (b + 1))
                    settle(sp)
            for par in range(2):
                sp.wait_ge(lo_stored[par], START + 16 * B * HALF)

            with sp.Fori(0, B) as b:
                sp.wait_ge(x3_stored, START + 16 * b)
                load_rows(xh, x[b], x_loaded)
                sp.wait_ge(x3_done, START + b)
                load_rows(tmp, y_dram[b], y_loaded)
                sp.wait_ge(gn_out, START + B + 3 * b + 1)
                sp.dma_start(plane_view(pad_zero, C)[1:H + 1], xn[:, :, :]).then_inc(xn_stored, 16)
                sp.wait_ge(norm_split, START + b + 1)
                sp.dma_start(plane_view(norm_parts, 3)[1:H + 1], rp[:, :, :]).then_inc(parts_stored, 16)
                sp.wait_ge(parts_stored, START + 16 * (b + 1))
                sp.wait_ge(filt_used, START + 2 * 8 * (b + 1))
                sp.dma_start(norms[0:BIAS_ROWS, :], bass.AP(tensor=ones_dram, offset=0, ap=[[H * PW, BIAS_ROWS], [1, H * PW]])).then_inc(norms_loaded, 16)
                for n, (_, part) in enumerate(PAIRS):
                    for dy in range(3):
                        r0 = BIAS_ROWS + TAPS * n + 3 * dy
                        sp.dma_start(norms[r0:r0 + 3, :],
                                     bass.AP(tensor=norm_parts, offset=part * PLANE + dy * PW, ap=[[1, 3], [1, H * PW]])).then_inc(norms_loaded, 16)
                sp.wait_ge(xn_stored, START + 16 * (B + 2 * b + 1))
                sp.wait_ge(chunk_mm, START + (B + b) * CHUNKS)
                for par in range(2):
                    load_stacks(pad_zero, par * CR, par, True)
                with sp.Fori(1, HALF) as i:
                    for par in range(2):
                        sp.wait_ge(mix_mm, START + MIX_CREDIT + (b * HALF + i) * PAIR_COMBOS - (1 - par) * COMBOS)
                        load_stacks(pad_zero, (2 * i + par) * CR, par, True)
                for par in range(2):
                    sp.wait_ge(lo_stored[par], START + 16 * (B * HALF + b * 2 * HALF + HALF))
                load_rows(tmp, l1_dram, branch_loaded)
                sp.wait_ge(x3_done, START + b + 1)
                sp.dma_start(x3_dram[b].rearrange("c h w -> h c w"), xh[:, :, :]).then_inc(x3_stored, 16)
                sp.wait_ge(gn_out, START + B + 3 * b + 3)
                sp.wait_ge(att_mul, START + b + 1)
                sp.dma_start(plane_view(pad_wrap, C)[1:H + 1], xn[:, :, :]).then_inc(xn_stored, 16)
                sp.dma_start(plane_view(pad_wrap, C)[0:1], xn[H - 1:H, :, :]).then_inc(border_done, 16)
                sp.dma_start(plane_view(pad_wrap, C)[H + 1:H + 2], xn[0:1, :, :]).then_inc(border_done, 16)
                sp.wait_ge(xn_stored, START + 16 * (B + 2 * b + 2))
                sp.wait_ge(border_done, START + 16 * (BORDERS + 2 * b + 2))
                sp.wait_ge(mix_mm, START + MIX_CREDIT + (b + 1) * HALF * PAIR_COMBOS)
                conv_stacks(pad_wrap, (B + b) * CHUNKS)
                for par in range(2):
                    sp.wait_ge(stack_loaded[par], START + LOAD1 * B + (LOADM + LOAD3) * (b + 1))
                    settle(sp)

            sp.wait_ge(chunk_mm, START + 2 * B * CHUNKS)
            for r, t, w in ((0, 0, w1r), (1, 0, w1i), (0, 1, w2r), (1, 1, w2i)):
                for q in range(4):
                    sp.dma_start(wm[C * q:C * q + C, r, t, :, :],
                                 w[:, :, 4 * q:4 * q + 4, :].rearrange("i o x y -> i o (x y)")).then_inc(wm_loaded, 16)
            sp.wait_ge(spec_copy, 8)
            for t in range(2):
                for q in range(4):
                    for xx in range(4):
                        sp.dma_start(spec_dram[MODES * t + 4 * q + xx],
                                     ys[C * q:C * q + C, 4 * t + xx, :, :].rearrange("p b m -> p (b m)")).then_inc(spec_stored, 16)
            sp.wait_ge(spec_stored, 16 * KX)
            sp.dma_start(normsf[0:KX, 0:C * B * 2 * MODES], spec_dram.rearrange("x o m -> x (o m)")).then_inc(spec_loaded, 16)
            for par in range(2):
                sp.wait_ge(lo_stored[par], START + 16 * 3 * B * HALF)

            with sp.Fori(0, B) as b:
                sp.wait_ge(x3_stored, START + 16 * B)
                sp.wait_ge(out_stored, START + 16 * b)
                load_rows(xh, x3_dram[b], x_loaded)
                load_rows(tmp, l3_dram[b], y_loaded)
                sp.wait_ge(out_done, START + 8 * (b + 1))
                sp.dma_start(out[b].rearrange("c h w -> h c w"), xh[:, :, :]).then_inc(out_stored, 16)
            sp.wait_ge(out_stored, START + 16 * B)

        @block.tensor
        def _(pe):
            def group_norm(n):
                pe.wait_ge(gn_stats, START + n + 1)
                for half, e in enumerate((1, 4)):
                    m = pe.matmul(ps[:, 0, 0:C], const("mean"), st[:, :, e], start=half == 0, stop=half == 1)
                m.then_inc(gn_mean, 1)
                pe.wait_ge(gn_dev, START + n + 1)
                for half in range(2):
                    m = pe.matmul(ps[:, 1, 0:C], const("var"), dev[:, :, half], start=half == 0, stop=half == 1)
                m.then_inc(gn_var, 1)

            def conv_terms(layer, par, last):
                for s in range(STACKS):
                    for g in range(G):
                        m = pe.matmul(ps[C * g:C * g + C, 6 + par, :], w_conv[:, layer, s, :],
                                      stack[:, par, s, g, :].rearrange("p (r w) -> p r w", w=PW)[:, :, 0:W],
                                      start=s == 0, stop=last and s == STACKS - 1)
                return m

            def conv_chunks(layer, chunk0, loaded0):
                with pe.Fori(0, HALF) as i:
                    for par in range(2):
                        pe.wait_ge(stack_loaded[par], START + loaded0 + 16 * NCONV_DMA * (i + 1))
                        pe.wait_ge(chunk_evac, START + chunk0 + 2 * i + par)
                        conv_terms(layer, par, True).then_inc(chunk_mm, 1)

            pe.wait_ge(const_loaded, 16)
            pe.wait_ge(par_loaded, 16 * PARS)
            pe.wait_ge(init_done, 2)
            with pe.Fori(0, B) as b:
                group_norm(b)
                conv_chunks(0, b * CHUNKS, b * LOAD1)

            pe.wait_ge(bn_dev, 1)
            pe.matmul(ps[:, 0, 0:1], const("same_o"), bagg[:, 0:1], start=True, stop=True).then_inc(bn_mat, 1)
            pe.wait_ge(bn_dev, 2)
            pe.matmul(ps[:, 1, 0:2 * C], const("quarter"), bexp[:, :], start=True, stop=True).then_inc(bn_mat, 1)
            pe.wait_ge(filt_ready, 1)
            pe.wait_ge(op_ready, 1)
            pe.wait_ge(bn_ready, 1)

            with pe.Fori(0, B) as b:
                pe.wait_ge(relu_done, START + b + 1)
                for n in range(8):
                    if n >= 2:
                        pe.wait_ge(filt_used, START + 16 * b + 2 * (n - 1))
                    else:
                        pe.wait_ge(filt_used, START + 16 * b)
                    for d in range(5):
                        pe.matmul(ps[:, 2 + n % 2, :], circ[:, d, :], yp[:, 4 * n:4 * n + 4, 4 - d:4 - d + W], start=d == 0, stop=d == 4)
                    for d in range(3):
                        m = pe.matmul(ps[:, 4 + n % 2, :], circ[:, 5 + d, :], yp[:, 4 * n:4 * n + 4, 4 - d:4 - d + W], start=d == 0, stop=d == 2)
                    m.then_inc(filt_mm, 1)
                group_norm(B + 3 * b)

                pe.wait_ge(norm_root, START + b + 1)
                pe.wait_ge(norms_loaded, START + 16 * 19 * (b + 1))

                def spread(i, c):
                    par, s = divmod(c, COMBOS)
                    for half in range(2):
                        n = 2 * c + half
                        pe.wait_ge(tanh_done, START + (b * HALF + i) * PAIR_ITEMS + n)
                        settle(pe)
                        for e in range(2):
                            g = 2 * half + e
                            rows = norms[0:KROWS, bass.ds(((2 * i + par) * CR + RB * g) * PW, SPAN)]
                            m = pe.matmul(ps[:, 2 * (n % 3) + e, :], opw[:, s, :],
                                          rows.rearrange("p (r w) -> p r w", w=PW)[:, :, 0:W], start=True, stop=True)
                        m.then_inc(spread_mm, 1)

                def mix(i, c):
                    par, s = divmod(c, COMBOS)
                    if s == 0:
                        pe.wait_ge(stack_loaded[par], START + B * LOAD1 + b * (LOADM + LOAD3) + 16 * NMIX_DMA * (i + 1))
                        pe.wait_ge(chunk_evac, START + (B + 2 * b) * CHUNKS + 2 * i + par)
                        conv_terms(1, par, False)
                    pool = sum(pool_item(n) for n in range(2 * c + 2))
                    pe.wait_ge(prod_dve, START + (b * HALF + i) * dve_items + 2 * c + 2 - pool)
                    if pool:
                        pe.wait_ge(prod_pool, START + (b * HALF + i) * pool_items + pool)
                    for g in range(G):
                        m = pe.matmul(ps[C * g:C * g + C, 6 + par, :], w_mix[:, s, :],
                                      ring[:, (2 * c + g // 2) % TRING, NPX * (g % 2):NPX * (g % 2) + NPX], start=False, stop=s == COMBOS - 1)
                    m.then_inc(mix_mm, 1)

                for c in range(LEAD):
                    spread(0, c)
                with pe.Fori(0, HALF - 1) as i:
                    for c in range(PAIR_COMBOS):
                        if c + LEAD < PAIR_COMBOS:
                            spread(i, c + LEAD)
                        else:
                            spread(i + 1, c + LEAD - PAIR_COMBOS)
                        mix(i, c)
                for c in range(PAIR_COMBOS):
                    if c + LEAD < PAIR_COMBOS:
                        spread(HALF - 1, c + LEAD)
                    mix(HALF - 1, c)
                group_norm(B + 3 * b + 1)

                pe.wait_ge(gray_done, START + b + 1)
                for d in range(5):
                    m = pe.matmul(ps[:, 2, 0:W], dogm[:, d, :], gray[:, d:d + W], start=d == 0, stop=d == 4)
                m.then_inc(dog_mm, 1)
                pe.wait_ge(dog_copy, START + b + 1)
                for n, d in enumerate((0, 2)):
                    m = pe.matmul(ps[:, 3, 0:W], sobm[:, n, :], dog[:, d:d + W], start=n == 0, stop=n == 1)
                for d in range(3):
                    m = pe.matmul(ps[:, 4, 0:W], sobm[:, 2 + d, :], dog[:, d:d + W], start=d == 0, stop=d == 2)
                m.then_inc(sob_mm, 1)
                group_norm(B + 3 * b + 2)

                pe.wait_ge(gn_out, START + B + 3 * b + 3)
                for c in range(C):
                    m = pe.matmul(ps[:, 2 + c // 8, 64 * (c % 8):64 * (c % 8) + 64], xn[:, c, 1:W + 1], const("dft_h"), start=True, stop=True)
                m.then_inc(dfth_mm, 1)
                pe.wait_ge(dfth_copy, START + b + 1)
                for t in range(2):
                    for xx in range(4):
                        for q in range(4):
                            for r in range(2):
                                at = (4 * t + xx) * 2 * MODES
                                m = pe.matmul(ps[C * q:C * q + C, 0, at:at + 2 * MODES], z[:, :, r, MODES * t + 4 * q + xx],
                                              dftw[:, r, :], start=r == 0, stop=r == 1)
                m.then_inc(dftw_mm, 1)
                conv_chunks(2, (B + 2 * b + 1) * CHUNKS, B * LOAD1 + b * (LOADM + LOAD3) + LOADM)

            pe.wait_ge(wm_loaded, 16 * 16)
            pe.wait_ge(dftw_copy, START + 3 * B)
            pe.wait_ge(chunk_evac, START + EVAC_CREDIT + 3 * B * CHUNKS)
            for slot in range(4):
                for m_ in range(32):
                    for q in range(4):
                        grp = (slot + q) % 4
                        x8, ky = 2 * grp + m_ // MODES, m_ % MODES
                        t, xx = divmod(x8, 4)
                        for r in range(2):
                            m = pe.matmul(ps[C * q:C * q + C, grp, 16 * m_:16 * m_ + 16], wm[C * q:C * q + C, r, t, :, xx * MODES + ky],
                                          cs[C * q:C * q + C, 1 - r:3 - r, t, xx, ky, :], start=r == 0, stop=r == 1)
            m.then_inc(spec_mm, 1)

            with pe.Fori(0, B) as b:
                pe.wait_ge(slice_done, START + b + 1)
                for half in range(2):
                    if half == 0:
                        pe.wait_ge(idfth_copy, START + 2 * b)
                    else:
                        pe.wait_ge(idfth_copy, START + 2 * b + 1)
                    settle(pe)
                    for n in range(4):
                        for q in range(4):
                            m = pe.matmul(ps[C * q:C * q + C, n // 2, 256 * (n % 2):256 * (n % 2) + 256], v2b[:, 4 * (4 * half + n) + q, :],
                                          const("idft_h", KX), start=True, stop=True)
                    m.then_inc(idfth_mm, 1)
                pe.wait_ge(idfth_copy, START + 2 * b + 2)
                for half in range(2):
                    if half == 0:
                        pe.wait_ge(out_mul, START + 8 * b)
                    else:
                        pe.wait_ge(out_mul, START + 8 * b + 4)
                    for n in range(4):
                        for q in range(4):
                            for s in range(2):
                                m = pe.matmul(ps[:, 4 + q, W * n:W * n + W], u[C * q:C * q + C, 4 * half + n, H * s:H * s + H],
                                              idftw[C * q:C * q + C, s, :], start=s == 0, stop=s == 1)
                    m.then_inc(idftw_mm, 1)

        @block.scalar
        def _(act):
            def group_norm(n):
                act.wait_ge(gn_var, START + n + 1)
                nc.scalar.activation(sd[:, :], ps[:, 1, 0:C], ACT.Sqrt, bias=eps[:, 0:1]).then_inc(gn_sd, 1)

            def evacuate(layer, par, chunk, stored, target):
                act.wait_ge(lo_stored[par], START + stored)
                nc.scalar.activation(lo[:, par, :], ps[:, 6 + par, :], ACT.Identity, bias=bias[:, layer:layer + 1]).then_inc(chunk_evac, 1)
                act.wait_ge(chunk_evac, START + EVAC_CREDIT + chunk + 1)
                act.dma_start(target, lo[:, par, :]).then_inc(lo_stored[par], 16)

            def rows_of(image, i, par):
                return image.rearrange("c (g r) w -> g c (r w)", g=G)[:, :, bass.ds((2 * i + par) * NPX, NPX)]

            def conv_chunks(layer, b, conv0, chunk0, stored0, image):
                with act.Fori(0, HALF) as i:
                    for par in range(2):
                        act.wait_ge(chunk_mm, START + conv0 + 2 * i + par + 1)
                        if layer == 0:
                            act.wait_ge(chunk_stat, START + chunk0 + 2 * i)
                        evacuate(layer, par, chunk0 + 2 * i + par, stored0 + 16 * i, rows_of(image, i, par))

            act.wait_ge(par_loaded, 16 * PARS)
            act.wait_ge(init_done, 2)
            with act.Fori(0, B) as b:
                group_norm(b)
                conv_chunks(0, b, b * CHUNKS, b * CHUNKS, 16 * b * HALF, y_dram[b])
            act.wait_ge(bn_act, 1)
            nc.scalar.activation(sd[:, :], bn_m[:, C:2 * C], ACT.Sqrt, bias=eps[:, 0:1]).then_inc(bn_sd, 1)

            with act.Fori(0, B) as b:
                act.wait_ge(bn_applied, START + b + 1)
                act.wait_ge(mix_mm, START + MIX_CREDIT + b * HALF * PAIR_COMBOS)
                nc.scalar.activation(yp[:, :, 4:YPW], tmp[:, :, :], ACT.Relu)
                nc.scalar.activation(yp[:, :, 0:4], tmp[:, :, W - 4:W], ACT.Relu).then_inc(relu_done, 1)
                for n in range(8):
                    act.wait_ge(filt_mm, START + 8 * b + n + 1)
                    if n >= 2:
                        act.wait_ge(filt_used, START + 16 * b + 2 * (n - 1))
                    nc.scalar.activation(sq[:, n % 2, :], ps[:, 4 + n % 2, :], ACT.Square).then_inc(filt_sq, 1)
                group_norm(B + 3 * b)

                act.wait_ge(gn_out, START + B + 3 * b + 1)
                nc.scalar.activation(tmp[:, :, :], xn[:, :, 1:W + 1], ACT.Square).then_inc(norm_sq, 1)
                act.wait_ge(norm_sum, START + b + 1)
                nc.scalar.activation(rn[:, :], r2[:, :], ACT.Sqrt).then_inc(norm_root, 1)

                def tanh_pair(i, first):
                    pair = b * HALF + i
                    for n in range(PAIR_ITEMS):
                        act.wait_ge(spread_mm, START + pair * PAIR_ITEMS + n + 1)
                        act.wait_ge(mix_mm, START + pair * PAIR_COMBOS + n // 2)
                        nc.scalar.activation(ring[:, n % TRING, :], ps[:, 2 * (n % 3):2 * (n % 3) + 2, :].rearrange("p a n -> p (a n)"),
                                             ACT.Tanh).then_inc(tanh_done, 1)
                        if n == 7 and not first:
                            mixed_out(i - 1, 1)
                        if n == ITEMS + 7:
                            mixed_out(i, 0)

                def mixed_out(i, par):
                    act.wait_ge(mix_mm, START + MIX_CREDIT + (b * HALF + i) * PAIR_COMBOS + (par + 1) * COMBOS)
                    evacuate(1, par, (B + 2 * b) * CHUNKS + 2 * i + par, 16 * ((B + 2 * b) * HALF + i), rows_of(l1_dram, i, par))

                tanh_pair(0, True)
                with act.Fori(1, HALF) as i:
                    tanh_pair(i, False)
                mixed_out(HALF - 1, 1)
                group_norm(B + 3 * b + 1)

                act.wait_ge(dog_mm, START + b + 1)
                nc.scalar.copy(dog[:, 1:W + 1], ps[:, 2, 0:W]).then_inc(dog_copy, 1)
                act.wait_ge(sob_mm, START + b + 1)
                nc.scalar.activation(r2[:, :], ps[:, 3, 0:W], ACT.Square)
                nc.scalar.activation(rn[:, :], ps[:, 4, 0:W], ACT.Square).then_inc(sob_sq, 1)
                act.wait_ge(mag_sum, START + b + 1)
                nc.scalar.activation(rn[:, :], ra[:, :], ACT.Sqrt, bias=eps[:, 1:2]).then_inc(att_act, 1)
                act.wait_ge(att_act, START + 2 * b + 1)
                nc.scalar.activation(r2[:, :], rn[:, :], ACT.Sigmoid, scale=gate[:, 0:1], bias=gate[:, 1:2]).then_inc(att_act, 1)
                group_norm(B + 3 * b + 2)

                act.wait_ge(dfth_mm, START + b + 1)
                for n in range(4):
                    m = nc.scalar.copy(z[:, 8 * n:8 * n + 8, :, :].rearrange("p c r x -> p (c r x)"), ps[:, 2 + n, :])
                m.then_inc(dfth_copy, 1)
                act.wait_ge(dftw_mm, START + b + 1)
                w_out = ps[:, 0, 0:8 * 2 * MODES].rearrange("p (x r y) -> p r x y", x=8, r=2)
                for n, (r, sign) in enumerate(((1, -1.0), (0, 1.0), (1, 1.0))):
                    nc.scalar.activation(cs[:, n, :, :, :, bass.ds(b, 1)].rearrange("p t x y b -> p (t x) (y b)"),
                                         w_out[:, r, :, :], ACT.Copy, scale=sign).then_inc(dftw_copy, 1)
                conv_chunks(2, b, (B + b) * CHUNKS, (B + 2 * b + 1) * CHUNKS, 16 * (B + 2 * b + 1) * HALF, l3_dram[b])

            act.wait_ge(spec_mm, 1)
            for n in range(8):
                src = ps[:, n // 2, 256 * (n % 2):256 * (n % 2) + 256].rearrange("p (y r b) -> p b r y", y=MODES, r=2)
                nc.scalar.copy(ys[:, n, :, :].rearrange("p b (r y) -> p b r y", r=2), src).then_inc(spec_copy, 1)

            act.wait_ge(spec_loaded, 16)
            act.wait_ge(spec_copy, 8)
            with act.Fori(0, B) as b:
                act.wait_ge(idfth_mm, START + 2 * b)
                nc.scalar.copy(v2b, v2[:, :, bass.ds(b, 1), :].rearrange("p o b m -> p (o b) m")).then_inc(slice_done, 1)
                for half in range(2):
                    act.wait_ge(idfth_mm, START + 2 * b + half + 1)
                    if half == 0:
                        act.wait_ge(idftw_mm, START + 2 * b)
                    for n in range(2):
                        m = nc.scalar.copy(u[:, 4 * half + 2 * n:4 * half + 2 * n + 2, :].rearrange("p a n -> p (a n)"), ps[:, n, :])
                    m.then_inc(idfth_copy, 1)

        @block.gpsimd
        def _(pool):
            for s in counted:
                pool.sem_inc(s, START)
            with pool.Fori(0, B) as b:
                with pool.Fori(0, HALF) as i:
                    for n in range(2 * ITEMS):
                        if not pool_item(n):
                            continue
                        par, s, half = n // ITEMS, n % ITEMS // 2, n % 2
                        pool.wait_ge(tanh_done, START + TANH_CREDIT + (b * HALF + i) * PAIR_ITEMS + n + 1)
                        pool.wait_ge(stack_loaded[par], START + B * LOAD1 + b * (LOADM + LOAD3) + 16 * NMIX_DMA * (i + 1))
                        pixels = stack[:, par, stack_of(s), 2 * half:2 * half + 2, :].rearrange("p g (r w) -> p (g r) w", w=PW)[:, :, 0:W]
                        slot = ring[:, n % TRING, :].rearrange("p (r w) -> p r w", w=W)
                        nc.gpsimd.tensor_tensor(slot, slot, pixels, ALU.mult).then_inc(prod_pool, 1)

        @block.vector
        def _(dve):
            def group_norm(n, t, free_xn):
                for c in range(C):
                    m = nc.vector.bn_stats(st[:, c, :], xh[:, c, :])
                m.then_inc(gn_stats, 1)
                dve.wait_ge(gn_mean, START + n + 1)
                t.inc(nc.vector.tensor_copy(mu[:, :], ps[:, 0, 0:C]))
                t.wait()
                for e, at in enumerate((1, 4)):
                    t.inc(nc.vector.tensor_tensor(dev2[:, :, e], st[:, :, at], mu[:, :], ALU.subtract))
                t.wait()
                t.inc(nc.vector.tensor_tensor(dev2[:, :, :], dev2[:, :, :], dev2[:, :, :], ALU.mult))
                t.wait()
                for e, at in enumerate((2, 5)):
                    m = nc.vector.scalar_tensor_tensor(out=dev[:, :, e], in0=dev2[:, :, e], scalar=float(W // 2), in1=st[:, :, at],
                                                       op0=ALU.mult, op1=ALU.add)
                m.then_inc(gn_dev, 1)
                dve.wait_ge(gn_sd, START + n + 1)
                t.inc(nc.vector.reciprocal(rstd[:, :], sd[:, :]))
                t.wait()
                free_xn()
                for c in range(C):
                    m = nc.vector.tensor_scalar(xn[:, c, 1:W + 1], xh[:, c, :], mu[:, c:c + 1], rstd[:, c:c + 1], ALU.subtract, ALU.mult)
                return m

            GN_TICKS = 5

            nc.vector.memset(tmp[:, 0, :], 0.0)
            nc.vector.memset(ones, 1.0)
            nc.vector.memset(rp[:, :, :], 0.0).then_inc(init_done, 1)
            nc.vector.memset(xn[:, :, :], 0.0)
            nc.vector.memset(gray[:, :], 0.0)
            nc.vector.memset(dog[:, :], 0.0)
            nc.vector.memset(eps[:, 0:1], GN_EPS).then_inc(chunk_evac, EVAC_CREDIT)
            nc.vector.memset(bsm[:, 0:1], 0.0).then_inc(tanh_done, TANH_CREDIT)
            nc.vector.memset(bsm[:, 1:2], 0.0).then_inc(mix_mm, MIX_CREDIT)
            nc.vector.memset(eps[:, 1:2], MAG_EPS).then_inc(init_done, 1)
            t = Ticks(dve, step)
            dve.wait_ge(const_loaded, 16)
            dve.wait_ge(par_loaded, 16 * PARS)
            parts = const("parts", KROWS)
            opf = opw[:, :, :].rearrange("p s n -> p (s n)")
            t.inc(nc.vector.tensor_copy(opf, op_in))
            t.wait()
            t.inc(nc.vector.tensor_tensor(op_in, op_in, opf, ALU.subtract))
            t.wait()
            t.inc(nc.vector.tensor_scalar(op_rest, opf, parts[:, 0:1], None, ALU.mult))
            t.wait()
            t.inc(nc.vector.tensor_copy(opf, op_in))
            t.wait()
            t.inc(nc.vector.tensor_tensor(op_in, op_in, opf, ALU.subtract))
            t.inc(nc.vector.scalar_tensor_tensor(out=op_rest, in0=opf, scalar=parts[:, 1:2], in1=op_rest, op0=ALU.mult, op1=ALU.add))
            t.wait()
            t.inc(nc.vector.scalar_tensor_tensor(out=opf, in0=op_in, scalar=parts[:, 2:3], in1=op_rest, op0=ALU.mult, op1=ALU.add))
            t.wait()
            nc.vector.memset(stackf, 0.0).then_inc(op_ready, 1)

            t.inc(nc.vector.tensor_tensor(f3[:, :], fil[:, 0:TAPS], fil[:, TAPS:], ALU.subtract))
            t.inc(nc.vector.memset(f5[:, :, :], 0.0))
            t.wait()
            t.inc(nc.vector.memset(f5[:, 0, 0:1], 1.0))
            t.wait()
            for f in range(2):
                fv = fil[:, TAPS * f:TAPS * f + TAPS].rearrange("p (a b) -> p a b", a=3)
                for a in range(3):
                    for c in range(3):
                        t.inc(nc.vector.scalar_tensor_tensor(out=f5[:, a:a + 3, c:c + 3], in0=fv, scalar=fv[:, a, c:c + 1],
                                                             in1=f5[:, a:a + 3, c:c + 3], op0=ALU.mult, op1=ALU.add))
                        t.wait()
            for d in range(8):
                for a in range(5 if d < 5 else 3):
                    s = f5[:, a, d:d + 1] if d < 5 else f3[:, 3 * a + d - 5:3 * a + d - 4]
                    if a == 0:
                        t.inc(nc.vector.tensor_scalar(circ[:, d, :], shift[:, a, :], s, None, ALU.mult))
                    else:
                        t.inc(nc.vector.scalar_tensor_tensor(out=circ[:, d, :], in0=shift[:, a, :], scalar=s, in1=circ[:, d, :],
                                                             op0=ALU.mult, op1=ALU.add))
                    t.wait()
            nc.vector.memset(ra[:, :], 0.0).then_inc(filt_ready, 1)
            n0 = t.n

            with dve.Fori(0, B) as b:
                t = Ticks(dve, step, n0 + GN_TICKS * b)
                dve.wait_ge(x_loaded, START + 32 * (b + 1))
                group_norm(b, t, lambda: dve.wait_ge(xn_stored, START + 16 * b)).then_inc(gn_out, 1)
                assert t.n == GN_TICKS
                with dve.Fori(0, CHUNKS) as i:
                    dve.wait_ge(chunk_evac, START + EVAC_CREDIT + b * CHUNKS + i + 1)
                    nc.vector.bn_stats(bst[:, bass.ds(b * CHUNKS + i, 1), :].rearrange("p a s -> p (a s)"),
                                       lo[:, bass.ds(i % 2, 1), :].rearrange("p a n -> p (a n)")).then_inc(chunk_stat, 1)
            n0 += GN_TICKS * B

            t = Ticks(dve, step, n0)
            dve.wait_ge(chunk_stat, START + B * CHUNKS)
            nc.vector.bn_aggr(bagg[:, :], bst[:, :, :].rearrange("p a s -> p (a s)")).then_inc(bn_dev, 1)
            dve.wait_ge(bn_mat, 1)
            t.inc(nc.vector.tensor_copy(bsm[:, 2:3], ps[:, 0, 0:1]))
            t.wait()
            dve.wait_ge(bn_dev, 1)
            t.inc(nc.vector.tensor_tensor(bsm[:, 3:4], bagg[:, 0:1], bsm[:, 2:3], ALU.subtract))
            t.wait()
            t.inc(nc.vector.tensor_tensor(bsm[:, 4:5], bsm[:, 3:4], bsm[:, 3:4], ALU.mult))
            t.wait()
            t.inc(nc.vector.tensor_tensor(bsm[:, 5:6], bsm[:, 4:5], bagg[:, 1:2], ALU.add))
            t.wait()
            nc.vector.tensor_scalar(bexp[:, 0:C], const("eye_o"), bsm[:, 2:3], None, ALU.mult)
            nc.vector.tensor_scalar(bexp[:, C:2 * C], const("eye_o"), bsm[:, 5:6], None, ALU.mult).then_inc(bn_dev, 1)
            dve.wait_ge(bn_mat, 2)
            nc.vector.tensor_copy(bn_m[:, :], ps[:, 1, 0:2 * C]).then_inc(bn_act, 1)
            dve.wait_ge(bn_act, 1)
            dve.wait_ge(bn_sd, 1)
            t.inc(nc.vector.reciprocal(rstd[:, :], sd[:, :]))
            t.wait()
            t.inc(nc.vector.tensor_tensor(bn_a[:, :], rstd[:, :], gam[:, 0:C], ALU.mult))
            t.wait()
            t.inc(nc.vector.tensor_tensor(bn_b[:, :], bn_m[:, 0:C], bn_a[:, :], ALU.mult))
            t.wait()
            t.inc(nc.vector.tensor_tensor(bn_b[:, :], gam[:, C:2 * C], bn_b[:, :], ALU.subtract))
            t.wait()
            nc.vector.memset(bsm[:, 6:7], 0.0).then_inc(bn_ready, 1)
            n0 += t.n

            PHASE2_TICKS = 3 * GN_TICKS + 8
            with dve.Fori(0, B) as b:
                t = Ticks(dve, step, n0 + PHASE2_TICKS * b)
                dve.wait_ge(y_loaded, START + 32 * (b + 1))
                for c in range(C):
                    m = nc.vector.tensor_scalar(tmp[:, c, :], tmp[:, c, :], bn_a[:, c:c + 1], bn_b[:, c:c + 1], ALU.mult, ALU.add)
                m.then_inc(bn_applied, 1)
                dve.wait_ge(x_loaded, START + 32 * (B + b + 1))
                for n in range(8):
                    dve.wait_ge(filt_mm, START + 8 * b + n + 1)
                    xs = xh[:, 4 * n:4 * n + 4, :].rearrange("p c w -> p (c w)")
                    nc.vector.tensor_tensor(xs, xs, ps[:, 2 + n % 2, :], ALU.add).then_inc(filt_used, 1)
                    dve.wait_ge(filt_sq, START + 8 * b + n + 1)
                    dve.wait_ge(filt_used, START + 16 * b + 2 * n + 1)
                    nc.vector.tensor_tensor(xs, xs, sq[:, n % 2, :], ALU.add).then_inc(filt_used, 1)
                dve.wait_ge(filt_used, START + 16 * (b + 1))
                def free1():
                    dve.wait_ge(xn_stored, START + 16 * (B + 2 * b))
                    dve.wait_ge(border_done, START + 16 * (BORDERS + 2 * b))
                    dve.wait_ge(dfth_mm, START + b)
                m = group_norm(B + 3 * b, t, free1)
                m.then_inc(step, 1)
                t.n += 1
                for col in (0, PW - 1):
                    m = nc.vector.memset(xn[:, :, col:col + 1], 0.0)
                m.then_inc(gn_out, 1)
                dve.wait_ge(norm_sq, START + b + 1)
                nc.vector.tensor_reduce(r2[:, :], tmp[:, :, :].rearrange("p c w -> p w c"), AX.X, ALU.add).then_inc(norm_sum, 1)
                dve.wait_ge(norm_root, START + b + 1)
                dve.wait_ge(parts_stored, START + 16 * b)
                t.inc(nc.vector.tensor_copy(rp[:, 0, 1:W + 1], rn[:, :]))
                t.wait()
                t.inc(nc.vector.tensor_tensor(ra[:, :], rn[:, :], rp[:, 0, 1:W + 1], ALU.subtract))
                t.wait()
                t.inc(nc.vector.tensor_copy(rp[:, 1, 1:W + 1], ra[:, :]))
                t.wait()
                t.inc(nc.vector.tensor_tensor(r2[:, :], ra[:, :], rp[:, 1, 1:W + 1], ALU.subtract))
                t.wait()
                nc.vector.tensor_copy(rp[:, 2, 1:W + 1], r2[:, :]).then_inc(norm_split, 1)
                with dve.Fori(0, HALF) as i:
                    for n in range(2 * ITEMS):
                        if pool_item(n):
                            continue
                        par, s, half = n // ITEMS, n % ITEMS // 2, n % 2
                        dve.wait_ge(tanh_done, START + TANH_CREDIT + (b * HALF + i) * PAIR_ITEMS + n + 1)
                        dve.wait_ge(stack_loaded[par], START + B * LOAD1 + b * (LOADM + LOAD3) + 16 * NMIX_DMA * (i + 1))
                        pixels = stack[:, par, stack_of(s), 2 * half:2 * half + 2, :].rearrange("p g (r w) -> p (g r) w", w=PW)[:, :, 0:W]
                        slot = ring[:, n % TRING, :].rearrange("p (r w) -> p r w", w=W)
                        nc.vector.tensor_tensor(slot, slot, pixels, ALU.mult).then_inc(prod_dve, 1)
                dve.wait_ge(branch_loaded, START + 32 * (b + 1))
                t.inc(nc.vector.tensor_tensor(xh[:, :, :], xh[:, :, :], tmp[:, :, :], ALU.add))
                t.wait()
                m = group_norm(B + 3 * b + 1, t, lambda: dve.wait_ge(xn_stored, START + 16 * (B + 2 * b + 1)))
                m.then_inc(gn_out, 1)
                dve.wait_ge(gn_out, START + B + 3 * b + 2)
                nc.vector.tensor_reduce(gray[:, 2:W + 2], xn[:, :, 1:W + 1].rearrange("p c w -> p w c"), AX.X, ALU.add).then_inc(gray_done, 1)
                dve.wait_ge(sob_sq, START + b + 1)
                nc.vector.tensor_tensor(ra[:, :], r2[:, :], rn[:, :], ALU.add).then_inc(mag_sum, 1)
                dve.wait_ge(att_act, START + 2 * b + 2)
                t.inc(nc.vector.tensor_scalar(ra[:, :], r2[:, :], 1.0, None, ALU.add))
                t.wait()
                gain = ra[:, :].rearrange("p (a w) -> p a w", a=1).to_broadcast([P, C, W])
                nc.vector.tensor_tensor(tmp[:, :, :], xn[:, :, 1:W + 1], gain, ALU.mult).then_inc(att_mul, 1)
                dve.wait_ge(att_mul, START + b + 1)
                nc.vector.tensor_tensor(xh[:, :, :], xh[:, :, :], tmp[:, :, :], ALU.add).then_inc(x3_done, 1)
                dve.wait_ge(x3_done, START + b + 1)
                m = group_norm(B + 3 * b + 2, t, lambda: None)
                t.inc(m)
                t.wait()
                nc.vector.tensor_copy(xn[:, :, 0:1], xn[:, :, W:W + 1])
                nc.vector.tensor_copy(xn[:, :, PW - 1:PW], xn[:, :, 1:2]).then_inc(gn_out, 1)
                assert t.n == PHASE2_TICKS, t.n
            n0 += PHASE2_TICKS * B

            with dve.Fori(0, B) as b:
                dve.wait_ge(x_loaded, START + 32 * (2 * B + b + 1))
                dve.wait_ge(y_loaded, START + 32 * (B + b + 1))
                for half in range(2):
                    dve.wait_ge(idftw_mm, START + 2 * b + half + 1)
                    for q in range(4):
                        def pick(tile):
                            return tile[:, 16 * half:16 * half + 16, :].rearrange("p (n q) w -> p n q w", q=4)[:, :, q, :]
                        g = ps[:, 4 + q, :].rearrange("p (n w) -> p n w", n=4)
                        nc.vector.tensor_tensor(pick(tmp), pick(tmp), g, ALU.mult).then_inc(out_mul, 1)
                        dve.wait_ge(out_mul, START + 8 * b + 4 * half + q + 1)
                        nc.vector.tensor_tensor(pick(xh), pick(xh), pick(tmp), ALU.add).then_inc(out_done, 1)


def _stacked(w_oikk):
    import numpy as np
    w = np.transpose(w_oikk.reshape(C, C, TAPS), (2, 1, 0))
    r = np.zeros((4, C, STACKS, C), w.dtype)
    for j in range(TAPS):
        r[j % 4, :, j // 4, :] = w[j]
    return r.reshape(P, STACKS, C)


def _constants():
    import numpy as np
    k = np.zeros((P, NCONST), np.float64)

    def put(name, a):
        lo, hi = CONST[name]
        k[:a.shape[0], lo:hi] = a

    h = np.arange(P)
    put("mean", np.full((P, P), 1.0 / (2 * H)))
    put("var", np.full((P, P), 1.0 / (H * W)))
    put("same_o", (h[:, None] % C == h[None, :] % C) / G)
    put("quarter", np.full((P, P), 1.0 / G))
    put("eye_o", (h[:, None] % C == np.arange(C)[None, :]) * 1.0)
    put("shift", np.concatenate([h[:, None] == (h[None, :] - a) % H for a in range(5)], 1) * 1.0)
    ax = np.arange(5) - 2.0
    g = [np.exp(-(ax[:, None] ** 2 + ax[None, :] ** 2) / (2.0 * s * s)) for s in (1.0, 2.0)]
    k5 = (g[0] / g[0].sum() - g[1] / g[1].sum()) / C
    band = lambda col, r: sum(col[d] * (h[:, None] == h[None, :] + d - r) for d in range(len(col)))
    put("dog", np.concatenate([band(k5[:, d], 2) for d in range(5)], 1))
    sob = [(-1, -2, -1), (1, 2, 1), (-1, 0, 1), (-2, 0, 2), (-1, 0, 1)]
    put("sobel", np.concatenate([band(c, 1) for c in sob], 1))
    kx = np.concatenate([np.arange(MODES), np.arange(H - MODES, H)])
    th = 2 * np.pi * np.outer(h, kx) / H
    put("dft_h", np.concatenate([np.cos(th), -np.sin(th)], 1))
    ky = np.arange(MODES)
    tw = 2 * np.pi * np.outer(h, ky) / W
    put("dft_w", np.concatenate([np.cos(tw), -np.sin(tw), np.sin(tw), np.cos(tw)], 1))
    put("idft_h", np.concatenate([np.cos(th.T), np.sin(th.T)], 1))
    a = (np.where(ky == 0, 1.0, 2.0) / (H * W))[:, None]
    cw, sw = a * np.cos(tw.T), a * np.sin(tw.T)
    put("idft_w", np.tile(np.concatenate([np.concatenate([cw, -sw], 0), np.concatenate([-sw, -cw], 0)], 1), (4, 1)))
    put("parts", np.array([[float(p == r) for p in range(3)] for r in range(BIAS_ROWS)]
                          + [[float(p == wp) for p in range(3)] for wp, _ in PAIRS for _ in range(TAPS)]))
    return k.astype(np.float32)


def kernel(**inputs):
    import numpy as np
    import concourse.bacc as _bacc
    from concourse.bass_utils import run_bass_kernel_spmd as _run

    v = {n: np.asarray(a) for n, a in inputs.items()}
    op_w, op_b = v["L1_conv_op_w"], v["L1_conv_op_b"]
    w1 = v["L1_conv_weight"].reshape(C, C, TAPS)
    op_rows = np.zeros((KROWS, COMBOS, 4, C), np.float32)
    mix = np.zeros((4, C, COMBOS, C), np.float32)
    for s in range(COMBOS):
        for q in range(4):
            if tap_pair(s, q) is None:
                continue
            j, kk = tap_pair(s, q)
            op_rows[:BIAS_ROWS, s, q, :] = op_b[TAPS * j + kk]
            for n in range(len(PAIRS)):
                op_rows[BIAS_ROWS + TAPS * n:BIAS_ROWS + TAPS * n + TAPS, s, q, :] = op_w[TAPS * j + kk][:, None]
            mix[q, :, s, :] = w1[:, :, kk]
    tile4 = lambda a: np.tile(a.reshape(C, 1), (G, 1))
    arrays = {
        "x": v["x"], "conv0_w": _stacked(v["L0_conv_conv_w"]), "conv0_b": tile4(v["L0_conv_conv_b"]),
        "bn_gamma": v["L0_conv_bn_gamma"], "bn_beta": v["L0_conv_bn_beta"],
        "filt_x": v["L0_conv_filt_x"].reshape(TAPS), "filt_y": v["L0_conv_filt_y"].reshape(TAPS),
        "conv1_w": _stacked(np.transpose(v["L1_conv_weight"], (1, 0, 2, 3))), "mix1_w": mix.reshape(P, COMBOS, C),
        "conv1_b": tile4(v["L1_conv_bias"]), "op_rows": op_rows.reshape(KROWS, COMBOS * P),
        "gate_w": v["L2_conv_gate_w"], "gate_b": v["L2_conv_gate_b"],
        "w1r": v["L3_conv_w1r"], "w1i": v["L3_conv_w1i"], "w2r": v["L3_conv_w2r"], "w2i": v["L3_conv_w2i"],
        "conv3_w": _stacked(v["L3_conv_conv_w"]), "conv3_b": tile4(v["L3_conv_conv_b"]), "consts": _constants(),
    }
    nc = _bacc.Bacc("TRN2", target_bir_lowering=False, num_devices=1)
    given, args = {}, []
    for name, a in arrays.items():
        a = np.ascontiguousarray(a)
        given["in_" + name] = a
        args.append(nc.dram_tensor("in_" + name, a.shape, mybir.dt.from_np(a.dtype), kind="ExternalInput").ap())
    args.append(nc.dram_tensor("out_0", (B, C, H, W), F32, kind="ExternalOutput").ap())
    four_layers(nc, *args)
    r = _run(nc, [given], core_ids=[0])
    return r.results[0]["out_0"]
```

```python
from contextlib import ExitStack

import concourse.bass as bass
from concourse import mybir

F32 = mybir.dt.float32
BF16 = mybir.dt.bfloat16
ALU = mybir.AluOpType
ACT = mybir.ActivationFunctionType
AX = mybir.AxisListType

B, C, H, W = 8, 32, 128, 128
P = 128
G = P // C
RB = H // G
PW = W + 2
PLANE = (H + 2) * PW
TAIL = 8
CR = 4
CHUNKS = RB // CR
SPAN = CR * PW
NPX = CR * W
TAPS = 9
STACKS = 3
COMBOS = 21
ITEMS = 2 * COMBOS
MODES = 16
KX = 2 * MODES
BIAS_ROWS = 3
PAIRS = [(0, 0), (1, 0), (2, 0), (0, 1), (1, 1), (0, 2)]
KROWS = BIAS_ROWS + TAPS * len(PAIRS)
GN_EPS = BN_EPS = 1e-5
MAG_EPS = 1e-6
TRING = 6
START = 1
NORM_SLOTS = ((14, 70), (143, 157))
EVAC_CREDIT = 1
TANH_CREDIT = 1
MIX_CREDIT = 2
SLOTS = CHUNKS * COMBOS
BATCH_ITEMS = 2 * SLOTS
LEAD = 2
QC = C // 4
CSPAN = (CR + 2) * PW
YPW = W + 4

CONST = {}
_at = 0
for _name, _n in (("mean", P), ("var", P), ("same_o", P), ("quarter", P), ("eye_o", C), ("dog", 5 * P),
                  ("sobel", 5 * P), ("dft_h", 2 * KX), ("dft_w", 4 * MODES), ("idft_w", W), ("idft_h", 2 * H), ("parts", 3)):
    CONST[_name] = (_at, _at + _n)
    _at += _n
NCONST = _at


def pool_item(i):
    if any(first <= i // 2 < last for first, last in NORM_SLOTS):
        return i % 2 == 1
    return i % 10 in (1, 4, 7)


def tap_pair(s, q):
    if s < 18:
        return (4 * (s // 9) + q, s % 9)
    k = 4 * (s - 18) + q
    return (8, k) if k < TAPS else None


def stack_of(s):
    return s // 9 if s < 18 else 2


class Ticks:

    def __init__(self, eng, sem, base=0):
        self.eng, self.sem, self.base, self.n = eng, sem, base, 0

    def inc(self, ins):
        ins.then_inc(self.sem, 1)
        self.n += 1
        return ins

    def wait(self):
        self.eng.wait_ge(self.sem, START + self.base + self.n)


def four_layers(nc, x, conv0_w, conv0_b, bn_gamma, bn_beta, filt_x, filt_y, conv1_w, mix1_w, conv1_b, op_rows,
                gate_w, gate_b, w1r, w1i, w2r, w2i, conv3_w, conv3_b, consts, out):
    def dram(name, shape, dt=F32):
        return nc.dram_tensor(name, shape, dt, kind="Internal")

    PADDED = C * PLANE + TAIL
    pad0 = dram("pad0", (B, PADDED))
    pad1 = dram("pad1", (B, PADDED))
    pad3 = dram("pad3", (B, PADDED))
    parts_dram = dram("parts_dram", (B, 3 * PLANE + TAIL), BF16)
    rows_dram = dram("rows_dram", (B, KROWS - BIAS_ROWS, H * PW), BF16)
    y_dram = dram("y_dram", (B, C, H, W)).ap()
    x1_dram = dram("x1_dram", (B, C, H, W)).ap()
    l1_dram = dram("l1_dram", (B, C, H, W)).ap()
    l3_dram = dram("l3_dram", (B, C, H, W)).ap()
    x3_dram = dram("x3_dram", (B, C, H, W)).ap()
    spec_dram = dram("spec_dram", (KX, C, B * 2 * MODES)).ap()

    def image_rows(t, b):
        flat = t.ap()[bass.ds(b, 1), 0:C * PLANE].rearrange("a (c h w) -> (a h) c w", c=C, w=PW)
        return flat

    def window(t, b, channels, first, n):
        planes = bass.AP(tensor=t, offset=0, ap=[[PADDED, B], [PLANE, channels], [RB * PW, G], [1, (RB - CR + 2) * PW + 2 + SPAN]])
        return planes[bass.ds(b, 1), :, :, bass.ds(first, n)].rearrange("a c g n -> (a c) g n")

    with ExitStack() as ctx:
        def sb(name, shape, dt=F32):
            return ctx.enter_context(nc.sbuf_tensor(name, shape, dt))

        def once(name):
            return ctx.enter_context(nc.semaphore(name))

        counted = []

        def sem(name):
            counted.append(once(name))
            return counted[-1]

        xh = sb("xh", [P, C, W])
        xn = sb("xn", [P, C, PW])
        tmp = sb("tmp", [P, C, W])
        ypb = sb("ypb", [P, C * YPW])
        stack = sb("stack", [P, 2, STACKS, G, SPAN])
        cstack = sb("cstack", [3 * C, G, CSPAN])
        norms = sb("norms", [P, 2, G, SPAN], BF16)
        ring = sb("ring", [P, TRING, 2 * NPX])
        lo = sb("lo", [P, 2, NPX])
        lo3 = sb("lo3", [P, NPX])
        sq = sb("sq", [P, NPX])
        k = sb("k", [P, NCONST])
        circ = sb("circ", [P, 8, P])
        opw = sb("opw", [P, COMBOS, P], BF16)
        w_mix = sb("w_mix", [P, COMBOS, C])
        w_conv1 = sb("w_conv1", [P, STACKS, C])
        w_conv = sb("w_conv", [3 * C, 2, 3, C])
        bias = sb("bias", [P, 3])
        st = sb("st", [P, C, 6])
        dev = sb("dev", [P, C, 2])
        dev2 = sb("dev2", [P, C, 2])
        mu = sb("mu", [P, C])
        sd = sb("sd", [P, C])
        rstd = sb("rstd", [P, C])
        powers = sb("powers", [P, C])
        bagg = sb("bagg", [P, 2])
        bsm = sb("bsm", [P, 8])
        bexp = sb("bexp", [P, 2 * C])
        bn_a = sb("bn_a", [P, C])
        bn_b = sb("bn_b", [P, C])
        bn_m = sb("bn_m", [P, 2 * C])
        gam = sb("gam", [P, 2 * C])
        fil = sb("fil", [P, 2 * TAPS])
        f3 = sb("f3", [P, 9])
        f5 = sb("f5", [P, 5, 5])
        gate = sb("gate", [P, 2])
        gate_h = sb("gate_h", [P, 2])
        r2 = sb("r2", [P, W])
        rn = sb("rn", [P, W])
        ra = sb("ra", [P, W])
        rp = sb("rp", [P, 3, PW], BF16)
        gray = sb("gray", [P, W + 4])
        dog = sb("dog", [P, W + 2])
        cs = sb("cs", [P, 3, 2, 4, MODES, B])
        ps = ctx.enter_context(nc.psum_tensor("ps", [P, 8, NPX], F32))
        SUM, SIDE = 4, 6

        yp = ypb[:, :].rearrange("p (c w) -> p c w", c=C)
        z = ypb[:, 0:C * 2 * KX].rearrange("p (c r x) -> p c r x", c=C, r=2)
        stackf = stack[:, :, :, :, :].rearrange("p a s g n -> p (a s g n)")
        ringf = ring[:, :, :].rearrange("p a n -> p (a n)")
        stack0 = [stackf[0:3 * C, G * CSPAN * n:G * CSPAN * (n + 1)].rearrange("p (g n) -> p g n", g=G) for n in range(4)]
        op_in = stackf[0:KROWS, 0:COMBOS * P]
        shift = ringf[:, 4096:4096 + 5 * P].rearrange("p (a n) -> p a n", a=5)
        bst = ringf[:, 5120:5120 + B * CHUNKS * 6].rearrange("p (n s) -> p n s", s=6)
        op_rest = ringf[0:KROWS, 0:COMBOS * P]
        wm = stackf[:, 0:4 * C * 64].rearrange("p (r t o m) -> p r t o m", r=2, t=2, o=C)
        ys = ringf[:, 0:2048].rearrange("p (a b m) -> p a b m", a=8, b=B)
        v2 = stackf[0:KX, 0:C * B * 2 * MODES].rearrange("p (o b m) -> p o b m", o=C, b=B)
        v2b = xn[0:KX, :, :].rearrange("p c w -> p (c w)")[:, 0:C * 2 * MODES].rearrange("p (o m) -> p o m", o=C)
        u = ringf[:, 2048:4096].rearrange("p (m n) -> p m n", m=C // 2)
        xh2 = ypb[:, 0:C * W].rearrange("p (c w) -> p c w", c=C)
        tmp2 = stackf[:, C * B * 2 * MODES:C * B * 2 * MODES + C * W].rearrange("p (c w) -> p c w", c=C)

        def const(name, rows=P):
            a, b = CONST[name]
            return k[0:rows, a:b]

        dogm = const("dog").rearrange("p (a n) -> p a n", a=5)
        sobm = const("sobel").rearrange("p (a n) -> p a n", a=5)
        dftw = const("dft_w").rearrange("p (r n) -> p r n", r=2)
        idftw = const("idft_w")

        class Norm:
            def __init__(self, name):
                self.stats, self.mean, self.dev, self.var, self.shifted, self.root, self.out = (
                    sem(f"{name}_{s}") for s in ("stats", "mean", "dev", "var", "shifted", "root", "out"))

        gn0, gn1, gn2, gn3 = Norm("gn0"), Norm("gn1"), Norm("gn2"), Norm("gn3")
        const_loaded, par_loaded, zero_ready, init_done, op_ready, filt_ready = (once(n) for n in (
            "const_loaded", "par_loaded", "zero_ready", "init_done", "op_ready", "filt_ready"))
        border_done = sem("border_done")
        step0, head_step, tail_step = sem("step0"), sem("head_step"), sem("tail_step")
        x_loaded, xn0_stored, conv0_mm, conv0_evac, conv0_stat = (sem(n) for n in ("x_loaded", "xn0_stored", "conv0_mm", "conv0_evac", "conv0_stat"))
        stack0_loaded = [sem(f"stack0_loaded{n}") for n in range(4)]
        y_stored = [sem("y_stored0"), sem("y_stored1")]
        bn_dev, bn_mat, bn_var, bn_sd, bn_ready = (once(n) for n in ("bn_dev", "bn_mat", "bn_var", "bn_sd", "bn_ready"))
        xh_loaded, y_loaded, bn_applied, relu_done, c5_mm, c3_mm, c3_sq, c5_used, c3_used = (sem(n) for n in (
            "xh_loaded", "y_loaded", "bn_applied", "relu_done", "c5_mm", "c3_mm", "c3_sq", "c5_used", "c3_used"))
        x1_stored, xn1_stored, norm_sq, norm_sum, norm_root, norm_split, parts_stored, rows_stored = (sem(n) for n in (
            "x1_stored", "xn1_stored", "norm_sq", "norm_sum", "norm_root", "norm_split", "parts_stored", "rows_stored"))
        norm_split_in = sem("norm_split_in")
        stack_loaded, norms_loaded = [sem("stack_loaded0"), sem("stack_loaded1")], [sem("norms_loaded0"), sem("norms_loaded1")]
        spread_mm, tanh_done, prod_dve, prod_pool, mix_mm, sum_evac = (sem(n) for n in (
            "spread_mm", "tanh_done", "prod_dve", "prod_pool", "mix_mm", "sum_evac"))
        l1_stored = [sem("l1_stored0"), sem("l1_stored1")]
        x1_loaded, l1_loaded, x2_done, gray_done, dog_mm, dog_copy, sob_mm, sob_sq, mag_sum, mag_root, att_tanh, gain_done = (sem(n) for n in (
            "x1_loaded", "l1_loaded", "x2_done", "gray_done", "dog_mm", "dog_copy", "sob_mm", "sob_sq", "mag_sum", "mag_root", "att_tanh", "gain_done"))
        att_mul, x3_done, x3_stored, xn3_stored, dfth_mm, dfth_copy, dftw_mm, dftw_copy = (sem(n) for n in (
            "att_mul", "x3_done", "x3_stored", "xn3_stored", "dfth_mm", "dfth_copy", "dftw_mm", "dftw_copy"))
        cstack_loaded, conv3_mm, conv3_evac, l3_stored = sem("cstack_loaded"), sem("conv3_mm"), sem("conv3_evac"), sem("l3_stored")
        wm_loaded, spec_mm, spec_copy, spec_stored, spec_loaded = (once(n) for n in ("wm_loaded", "spec_mm", "spec_copy", "spec_stored", "spec_loaded"))
        x3_loaded, l3_loaded = [sem("x3_loaded0"), sem("x3_loaded1")], [sem("l3_loaded0"), sem("l3_loaded1")]
        slice_done, idfth_mm, idfth_copy, idftw_mm, out_mul, out_done = (sem(n) for n in (
            "slice_done", "idfth_mm", "idfth_copy", "idftw_mm", "out_mul", "out_done"))
        out_stored = [sem("out_stored0"), sem("out_stored1")]

        def settle(eng):
            eng.nop(nofuse=True)

        block = ctx.enter_context(nc.Block())

        PARS = 14
        BORDERS = (2 * (2 * 2 + 1) + 4) * B
        HALF = CHUNKS // 2
        pool_items = sum(pool_item(n) for n in range(BATCH_ITEMS))
        dve_items = BATCH_ITEMS - pool_items
        LOAD_STACK = 16 * 4 * STACKS
        LOAD_CONV = 16 * 3

        X2_SLOT, NORM2_SLOT, GRAY_SLOT, ATT_SLOT = 14, 18, 31, 42
        NORM3_SLOT, DFT_SLOT = 50, 62
        BN_SLOT, RELU_SLOT, FILT_SLOT, FILT_STEP = 64, 71, 75, 8
        NORM1_SLOT, CHAN_SLOT = 141, 151
        NEXT_SLOT = 158

        @block.sync
        def _(sp):
            def rows_in(tile, image, loaded):
                rows = image.rearrange("a c h w -> (a h) c w")
                for h0 in (0, H // 2):
                    sp.dma_start(tile[h0:h0 + H // 2, :, :], rows[h0:h0 + H // 2]).then_inc(loaded, 16)

            def at(t, b):
                return t[bass.ds(b, 1)]

            def conv_window(dst, src, b, chunk, loaded):
                for dx in range(3):
                    sp.dma_start(dst[C * dx:C * dx + C, :, :], window(src, b, C, chunk * CR * PW + dx, CSPAN)).then_inc(loaded, 16)

            def layer1_chunk(b, chunk):
                par = chunk % 2
                for j in range(4 * STACKS):
                    s, q = divmod(j, 4)
                    dy, dx = divmod(min(j, 8), 3)
                    sp.dma_start(stack[C * q:C * q + C, par, s, :, :],
                                 window(pad1, b, C, (chunk * CR + dy) * PW + dx, SPAN)).then_inc(stack_loaded[par], 16)
                rows = rows_dram.ap()[bass.ds(b, 1)].rearrange("a k (g n) -> (a k) g n", g=G)
                sp.dma_start(norms[BIAS_ROWS:KROWS, par, :, :], rows[:, :, chunk * SPAN:chunk * SPAN + SPAN]).then_inc(norms_loaded[par], 16)

            sp.dma_start(k[:, :], consts[:, 0:NCONST]).then_inc(const_loaded, 16)
            sp.dma_start(ringf[:, 4096:4096 + 5 * P], consts[:, NCONST:NCONST + 5 * P]).then_inc(const_loaded, 16)
            for dst, src in ((op_in, op_rows), (w_mix[:, :, :], mix1_w), (w_conv[:, 0, :, :], conv0_w), (w_conv1[:, :, :], conv1_w),
                             (w_conv[:, 1, :, :], conv3_w), (bias[:, 0:1], conv0_b), (bias[:, 1:2], conv1_b), (bias[:, 2:3], conv3_b),
                             (gam[:, 0:C], bn_gamma.partition_broadcast(P)), (gam[:, C:2 * C], bn_beta.partition_broadcast(P)),
                             (fil[:, 0:TAPS], filt_x.partition_broadcast(P)), (fil[:, TAPS:], filt_y.partition_broadcast(P)),
                             (gate[:, 0:1], gate_w.partition_broadcast(P)), (gate[:, 1:2], gate_b.partition_broadcast(P))):
                sp.dma_start(dst, src).then_inc(par_loaded, 16)
            rows_in(xh, at(x, 0), x_loaded)
            sp.wait_ge(zero_ready, 1)
            for b in range(B):
                for row in (0, H + 1):
                    for c0, n in ((0, W), (W, PW - W)):
                        for pad in (pad0, pad1):
                            sp.dma_start(image_rows(pad, b)[row, :, c0:c0 + n], tmp[0:C, 0, 0:n]).then_inc(border_done, 16)
                    sp.dma_start(bass.AP(tensor=parts_dram, offset=b * (3 * PLANE + TAIL) + row * PW, ap=[[PLANE, 3], [1, PW]]),
                                 rp[0:3, 0, :]).then_inc(border_done, 16)
                for pad in (pad0, pad1, pad3):
                    sp.dma_start(pad.ap()[b:b + 1, C * PLANE:PADDED], tmp[0:1, 0, 0:TAIL]).then_inc(border_done, 16)
                sp.dma_start(parts_dram.ap()[b:b + 1, 3 * PLANE:], rp[0:1, 0, 0:TAIL]).then_inc(border_done, 16)
            sp.wait_ge(border_done, START + 16 * BORDERS)
            sp.wait_ge(op_ready, 1)

            def store_padded0(b):
                sp.wait_ge(gn0.out, START + b + 1)
                sp.dma_start(image_rows(pad0, b)[1:H + 1], xn[:, :, :]).then_inc(xn0_stored, 16)

            def pass1(b, last):
                sp.wait_ge(xn0_stored, START + 16 * (b + 1))
                settle(sp)
                for chunk in range(CHUNKS):
                    if chunk < 4:
                        sp.wait_ge(conv0_mm, START + b * CHUNKS)
                    else:
                        sp.wait_ge(conv0_mm, START + b * CHUNKS + chunk - 3)
                    conv_window(stack0[chunk % 4], pad0, b, chunk, stack0_loaded[chunk % 4])
                    if chunk == 3 and not last:
                        rows_in(xh, at(x, b + 1), x_loaded)
                if not last:
                    store_padded0(b + 1)

            store_padded0(0)
            with sp.Fori(0, B - 1) as b:
                pass1(b, False)
            pass1(B - 1, True)
            for par in range(2):
                sp.wait_ge(y_stored[par], START + 16 * B * HALF)

            def load_y(h):
                rows_in(tmp, at(y_dram, h), y_loaded)

            def load_x(h):
                rows_in(xh, at(x, h), xh_loaded)

            def store_x1(h):
                sp.wait_ge(gn1.stats, START + h + 1)
                sp.dma_start(x1_dram[bass.ds(h, 1)].rearrange("a c h w -> (a h) c w"), xh[:, :, :]).then_inc(x1_stored, 16)

            def store_xn1(h):
                sp.wait_ge(gn1.out, START + h + 1)
                sp.dma_start(image_rows(pad1, h)[1:H + 1], xn[:, :, :]).then_inc(xn1_stored, 16)

            def store_norms(h):
                sp.wait_ge(norm_split, START + h + 1)
                own = parts_dram.ap()[bass.ds(h, 1), 0:3 * PLANE].rearrange("a (c h w) -> (a h) c w", c=3, w=PW)
                sp.dma_start(own[1:H + 1], rp[:, :, :]).then_inc(parts_stored, 16)

            def spread_norms(h):
                sp.wait_ge(parts_stored, START + 16 * (h + 1))
                settle(sp)
                shifted = bass.AP(tensor=parts_dram, offset=0, ap=[[3 * PLANE + TAIL, B], [1, 3], [1, 2 * PLANE + 2 * PW + H * PW]])
                for n, (_, part) in enumerate(PAIRS):
                    for dy in range(3):
                        r0 = TAPS * n + 3 * dy
                        first = part * PLANE + dy * PW
                        sp.dma_start(rows_dram.ap()[bass.ds(h, 1), r0:r0 + 3].rearrange("a k n -> (a k) n"),
                                     shifted[bass.ds(h, 1), :, first:first + H * PW].rearrange("a k n -> (a k) n")).then_inc(rows_stored, 16)

            def first_chunk(h):
                sp.wait_ge(xn1_stored, START + 16 * (h + 1))
                sp.wait_ge(rows_stored, START + 16 * 18 * (h + 1))
                settle(sp)
                layer1_chunk(h, 0)

            def tail_loads(t, heads):
                for par in range(2):
                    sp.wait_ge(l1_stored[par], START + 16 * HALF * (t + 1))
                sp.wait_ge(x1_stored, START + 16 * heads)
                sp.wait_ge(norm_sum, START + 4 * heads)
                settle(sp)
                rows_in(xh, at(x1_dram, t), x1_loaded)
                rows_in(tmp, at(l1_dram, t), l1_loaded)

            def store_x3(t):
                sp.wait_ge(x3_done, START + 4 * (t + 1))
                sp.dma_start(x3_dram[bass.ds(t, 1)].rearrange("a c h w -> (a h) c w"), xh[:, :, :]).then_inc(x3_stored, 16)

            def store_xn3(t):
                sp.wait_ge(gn3.out, START + t + 1)
                sp.dma_start(image_rows(pad3, t)[1:H + 1], xn[:, :, :]).then_inc(xn3_stored, 16)
                sp.dma_start(image_rows(pad3, t)[0:1], xn[H - 1:H, :, :]).then_inc(xn3_stored, 16)
                sp.dma_start(image_rows(pad3, t)[H + 1:H + 2], xn[0:1, :, :]).then_inc(xn3_stored, 16)

            def conv3_chunk(t, chunk):
                if chunk == 0:
                    sp.wait_ge(xn3_stored, START + 48 * (t + 1))
                sp.wait_ge(conv3_mm, START + t * CHUNKS + chunk)
                settle(sp)
                conv_window(cstack, pad3, t, chunk, cstack_loaded)

            def head_alone(h):
                load_y(h)
                load_x(h)
                store_x1(h)
                store_xn1(h)
                store_norms(h)
                spread_norms(h)
                first_chunk(h)

            def tail_steps(t, c, heads):
                if c == 5:
                    tail_loads(t, heads)
                if c == NORM3_SLOT:
                    store_x3(t)
                if c == DFT_SLOT:
                    store_xn3(t)
                if c >= FILT_SLOT - 5 and (c - FILT_SLOT + 5) % FILT_STEP == 0 and (c - FILT_SLOT + 5) // FILT_STEP < CHUNKS:
                    conv3_chunk(t, (c - FILT_SLOT + 5) // FILT_STEP)

            def head_steps(h, c):
                if c == NORM3_SLOT + 1:
                    sp.wait_ge(x3_done, START + 4 * (h - 1))
                    sp.wait_ge(x1_stored, START + 16 * h)
                    settle(sp)
                    load_y(h)
                if c == DFT_SLOT + 1:
                    sp.wait_ge(x3_stored, START + 16 * (h - 1))
                    sp.wait_ge(gn3.out, START + h - 1)
                    settle(sp)
                    load_x(h)
                if c == NORM1_SLOT + 1:
                    store_x1(h)
                if c == CHAN_SLOT - 1:
                    store_xn1(h)
                if c == CHAN_SLOT + 4:
                    store_norms(h)
                    spread_norms(h)
                if c == NEXT_SLOT:
                    sp.wait_ge(mix_mm, START + MIX_CREDIT + h * SLOTS - COMBOS)
                    first_chunk(h)

            def layer1(b, tail, head):
                for c in range(SLOTS):
                    if c % COMBOS == 0 and c // COMBOS + 1 < CHUNKS:
                        chunk = c // COMBOS + 1
                        if b is not None:
                            sp.wait_ge(mix_mm, START + MIX_CREDIT + b * SLOTS + (chunk - 1) * COMBOS)
                            settle(sp)
                        layer1_chunk(b, chunk)
                    if tail:
                        tail_steps(b - 1, c, b + 1)
                    if head:
                        head_steps(b + 1, c)

            head_alone(0)
            layer1(0, False, True)
            with sp.Fori(1, B - 1) as b:
                layer1(b, True, True)
            layer1(B - 1, True, False)
            sp.wait_ge(mix_mm, START + MIX_CREDIT + B * SLOTS)
            for r, t, w in ((0, 0, w1r), (1, 0, w1i), (0, 1, w2r), (1, 1, w2i)):
                for q in range(4):
                    sp.dma_start(wm[C * q:C * q + C, r, t, :, :],
                                 w[:, :, 4 * q:4 * q + 4, :].rearrange("i o x y -> i o (x y)")).then_inc(wm_loaded, 16)
            for c in range(SLOTS):
                tail_steps(B - 1, c, B)

            sp.wait_ge(spec_copy, 8)
            for t in range(2):
                for q in range(4):
                    for xx in range(4):
                        sp.dma_start(spec_dram[MODES * t + 4 * q + xx],
                                     ys[C * q:C * q + C, 4 * t + xx, :, :].rearrange("p b m -> p (b m)")).then_inc(spec_stored, 16)
            sp.wait_ge(spec_stored, 16 * KX)
            sp.dma_start(stackf[0:KX, 0:C * B * 2 * MODES], spec_dram.rearrange("x o m -> x (o m)")).then_inc(spec_loaded, 16)
            sp.wait_ge(l3_stored, START + 16 * B * CHUNKS)
            sp.wait_ge(x3_stored, START + 16 * B)

            with sp.Fori(0, B // 2) as i:
                for par, (xt, lt) in enumerate(((xh, tmp), (xh2, tmp2))):
                    sp.wait_ge(out_stored[par], START + 16 * i)
                    settle(sp)
                    rows_in(xt, at(x3_dram, 2 * i + par), x3_loaded[par])
                    rows_in(lt, at(l3_dram, 2 * i + par), l3_loaded[par])
                for par, (xt, lt) in enumerate(((xh, tmp), (xh2, tmp2))):
                    sp.wait_ge(out_done, START + 8 * (2 * i + par + 1))
                    settle(sp)
                    sp.dma_start(out[bass.ds(2 * i + par, 1)].rearrange("a c h w -> (a h) c w"), xt[:, :, :]).then_inc(out_stored[par], 16)
            for par in range(2):
                sp.wait_ge(out_stored[par], START + 16 * B // 2)

        @block.tensor
        def _(pe):
            def group_means(gn, n):
                pe.wait_ge(gn.stats, START + n + 1)
                for half, e in enumerate((1, 4)):
                    m = pe.matmul(ps[:, SIDE, 0:C], const("mean"), st[:, :, e], start=half == 0, stop=half == 1)
                m.then_inc(gn.mean, 1)

            def group_vars(gn, n):
                pe.wait_ge(gn.dev, START + n + 1)
                for half in range(2):
                    m = pe.matmul(ps[:, SIDE, 0:C], const("var"), dev[:, :, half], start=half == 0, stop=half == 1)
                m.then_inc(gn.var, 1)

            def conv(layer, tile, bank, done, rows=(0, 1, 2)):
                for dy in rows:
                    for g in range(G):
                        m = pe.matmul(ps[C * g:C * g + C, bank, :], w_conv[:, layer, dy, :],
                                      tile[:, g, dy * PW:(dy + CR) * PW].rearrange("p (r w) -> p r w", w=PW)[:, :, 0:W],
                                      start=dy == 0, stop=dy == 2)
                if rows[-1] == 2:
                    m.then_inc(done, 1)

            pe.wait_ge(const_loaded, 32)
            pe.wait_ge(par_loaded, 16 * PARS)
            pe.wait_ge(init_done, 1)

            def pass1(b, last):
                for chunk in range(CHUNKS):
                    pe.wait_ge(stack0_loaded[chunk % 4], START + LOAD_CONV * (2 * b + chunk // 4 + 1))
                    pe.wait_ge(conv0_evac, START + b * CHUNKS + chunk)
                    conv(0, stack0[chunk % 4], SUM + chunk % 2, conv0_mm)
                    if chunk == 4 and not last:
                        group_means(gn0, b + 1)
                        group_vars(gn0, b + 1)

            group_means(gn0, 0)
            group_vars(gn0, 0)
            with pe.Fori(0, B - 1) as b:
                pass1(b, False)
            pass1(B - 1, True)

            pe.wait_ge(bn_dev, 1)
            pe.matmul(ps[:, 0, 0:1], const("same_o"), bagg[:, 0:1], start=True, stop=True).then_inc(bn_mat, 1)
            pe.wait_ge(bn_dev, 2)
            pe.matmul(ps[:, 1, 0:2 * C], const("quarter"), bexp[:, :], start=True, stop=True).then_inc(bn_mat, 1)
            pe.wait_ge(filt_ready, 1)
            pe.wait_ge(op_ready, 1)
            pe.wait_ge(bn_ready, 1)

            def filter5(h, n, d0, d1):
                if d0 == 0:
                    pe.wait_ge(relu_done, START + 4 * h + n // 2 + 1)
                    pe.wait_ge(c5_used, START + 8 * h + n)
                for d in range(d0, d1):
                    m = pe.matmul(ps[:, SIDE, :], circ[:, d, :], yp[:, 4 * n:4 * n + 4, 4 - d:4 - d + W], start=d == 0, stop=d == 4)
                if d1 == 5:
                    m.then_inc(c5_mm, 1)

            def filter3(h, n, d0, d1, after):
                if d0 == 0:
                    pe.wait_ge(c3_sq, START + 8 * h + n)
                    if after is not None:
                        pe.wait_ge(conv3_evac, START + after)
                for d in range(d0, d1):
                    m = pe.matmul(ps[:, SIDE + 1, :], circ[:, 5 + d, :], yp[:, 4 * n:4 * n + 4, 4 - d:4 - d + W], start=d == 0, stop=d == 2)
                if d1 == 3:
                    m.then_inc(c3_mm, 1)

            def conv3_chunk(t, chunk, dy, head):
                if dy == 0:
                    pe.wait_ge(cstack_loaded, START + LOAD_CONV * (t * CHUNKS + chunk + 1))
                    if head is not None:
                        pe.wait_ge(c3_sq, START + 8 * head + chunk)
                    pe.wait_ge(conv3_evac, START + t * CHUNKS + chunk)
                conv(1, cstack, SIDE + 1, conv3_mm, (dy,))

            def blur(t):
                pe.wait_ge(gray_done, START + 4 * (t + 1))
                for d in range(5):
                    m = pe.matmul(ps[:, SIDE + 1, 0:W], dogm[:, d, :], gray[:, d:d + W], start=d == 0, stop=d == 4)
                m.then_inc(dog_mm, 1)

            def sobel(t):
                pe.wait_ge(dog_copy, START + t + 1)
                for n, d in enumerate((0, 2)):
                    m = pe.matmul(ps[:, SIDE, 0:W], sobm[:, n, :], dog[:, d:d + W], start=n == 0, stop=n == 1)
                for d in range(3):
                    m = pe.matmul(ps[:, SIDE + 1, 0:W], sobm[:, 2 + d, :], dog[:, d:d + W], start=d == 0, stop=d == 2)
                m.then_inc(sob_mm, 1)

            def dft_rows(t, n):
                if n == 0:
                    pe.wait_ge(gn3.out, START + t + 1)
                pe.wait_ge(dfth_copy, START + 4 * t + n)
                for c in range(QC * n, QC * n + QC):
                    at = 2 * KX * (c % QC)
                    m = pe.matmul(ps[:, SIDE, at:at + 2 * KX], xn[:, c, 1:W + 1], const("dft_h"), start=True, stop=True)
                m.then_inc(dfth_mm, 1)

            def dft_columns(t):
                pe.wait_ge(dfth_copy, START + 4 * (t + 1))
                for half in range(2):
                    for xx in range(4):
                        for q in range(4):
                            for r in range(2):
                                at = (4 * half + xx) * 2 * MODES
                                m = pe.matmul(ps[C * q:C * q + C, SIDE, at:at + 2 * MODES], z[:, :, r, MODES * half + 4 * q + xx],
                                              dftw[:, r, :], start=r == 0, stop=r == 1)
                m.then_inc(dftw_mm, 1)

            def head_steps(h, c, conv0):
                n, part = divmod(c - FILT_SLOT, FILT_STEP)
                if 0 <= n < 8 and part < 5:
                    if c == FILT_SLOT and conv0 is not None:
                        pe.wait_ge(dftw_copy, START + 3 * (h - 1))
                    filter5(h, n, part, part + 1)
                if 0 <= n < 8 and part >= 5:
                    filter3(h, n, part - 5, part - 4, None if conv0 is None else conv0 + n + 1)
                if c == NORM1_SLOT + 2:
                    pe.wait_ge(c5_used, START + 8 * (h + 1))
                    group_means(gn1, h)
                if c == NORM1_SLOT + 3:
                    group_vars(gn1, h)

            def tail_steps(t, c, head):
                if c == NORM2_SLOT + 5:
                    group_means(gn2, t)
                if c == NORM2_SLOT + 6:
                    group_vars(gn2, t)
                if c == GRAY_SLOT + 5:
                    blur(t)
                if c == GRAY_SLOT + 7:
                    sobel(t)
                if c == NORM3_SLOT + 5:
                    group_means(gn3, t)
                if c == NORM3_SLOT + 6:
                    group_vars(gn3, t)
                if c >= DFT_SLOT and (c - DFT_SLOT) % 2 == 0 and (c - DFT_SLOT) // 2 < 4:
                    dft_rows(t, (c - DFT_SLOT) // 2)
                if c == DFT_SLOT + 8:
                    dft_columns(t)
                n, part = divmod(c - FILT_SLOT, FILT_STEP)
                if 0 <= n < CHUNKS and part in (1, 2, 3):
                    conv3_chunk(t, n, part - 1, head)

            def layer1(b, tail, head):
                def spread(b, c, halves=(0, 1)):
                    chunk, s = divmod(c, COMBOS)
                    par = chunk % 2
                    if s == 0 and 0 in halves:
                        pe.wait_ge(norms_loaded[par], START + 16 * (b * HALF + chunk // 2 + 1))
                    for half in halves:
                        n = 2 * c + half
                        pe.wait_ge(tanh_done, START + b * BATCH_ITEMS + n)
                        settle(pe)
                        for e in range(2):
                            m = pe.matmul(ps[:, 2 * half + e, :], opw[:, s, :],
                                          norms[:, par, 2 * half + e, :].rearrange("p (r w) -> p r w", w=PW)[:, :, 0:W], start=True, stop=True)
                        m.then_inc(spread_mm, 1)

                def mix(c):
                    chunk, s = divmod(c, COMBOS)
                    par = chunk % 2
                    if s == 0:
                        pe.wait_ge(stack_loaded[par], START + LOAD_STACK * (b * HALF + chunk // 2 + 1))
                        pe.wait_ge(sum_evac, START + b * CHUNKS + chunk)
                        for n in range(STACKS):
                            for g in range(G):
                                pe.matmul(ps[C * g:C * g + C, SUM + par, :], w_conv1[:, n, :],
                                          stack[:, par, n, g, :].rearrange("p (r w) -> p r w", w=PW)[:, :, 0:W], start=n == 0, stop=False)
                    pool = sum(pool_item(n) for n in range(2 * c + 2))
                    pe.wait_ge(prod_dve, START + b * dve_items + 2 * c + 2 - pool)
                    pe.wait_ge(prod_pool, START + b * pool_items + pool)
                    for g in range(G):
                        m = pe.matmul(ps[C * g:C * g + C, SUM + par, :], w_mix[:, s, :],
                                      ring[:, (2 * c + g // 2) % TRING, NPX * (g % 2):NPX * (g % 2) + NPX], start=False, stop=s == COMBOS - 1)
                    m.then_inc(mix_mm, 1)

                if not tail:
                    for c in range(LEAD):
                        spread(b, c)
                for c in range(SLOTS):
                    for half in range(2):
                        if c + LEAD < SLOTS:
                            spread(b, c + LEAD, (half,))
                        elif head:
                            spread(b + 1, c + LEAD - SLOTS, (half,))
                        if head and half == 0:
                            head_steps(b + 1, c, (b - 1) * CHUNKS if tail else None)
                    if tail:
                        tail_steps(b - 1, c, b + 1 if head else None)
                    mix(c)

            for c in range(SLOTS):
                head_steps(0, c, None)
            layer1(0, False, True)
            with pe.Fori(1, B - 1) as b:
                layer1(b, True, True)
            layer1(B - 1, True, False)
            def mix_spectrum(turn, frequencies):
                for m_ in frequencies:
                    for q in range(4):
                        grp = (turn + q) % 4
                        x8, ky = 2 * grp + m_ // MODES, m_ % MODES
                        t, xx = divmod(x8, 4)
                        for r in range(2):
                            m = pe.matmul(ps[C * q:C * q + C, grp, 16 * m_:16 * m_ + 16], wm[C * q:C * q + C, r, t, :, xx * MODES + ky],
                                          cs[C * q:C * q + C, 1 - r:3 - r, t, xx, ky, :], start=r == 0, stop=r == 1)
                return m

            for c in range(FILT_SLOT):
                tail_steps(B - 1, c, None)
            pe.wait_ge(wm_loaded, 16 * 16)
            pe.wait_ge(dftw_copy, START + 3 * B)
            pe.wait_ge(sum_evac, START + EVAC_CREDIT + B * CHUNKS)
            for chunk in range(CHUNKS):
                for dy in range(3):
                    conv3_chunk(B - 1, chunk, dy, None)
                m = mix_spectrum(chunk // 2, range(16 * (chunk % 2), 16 * (chunk % 2) + 16))
            m.then_inc(spec_mm, 1)

            with pe.Fori(0, B) as b:
                pe.wait_ge(slice_done, START + b + 1)
                for half in range(2):
                    if half == 0:
                        pe.wait_ge(idfth_copy, START + 2 * b)
                    settle(pe)
                    for j in range(8 * half, 8 * half + 8):
                        for q in range(4):
                            c, s = 2 * j + q // 2, q % 2
                            m = pe.matmul(ps[C * q:C * q + C, j // 4, H * (j % 4):H * (j % 4) + H], v2b[:, c, :],
                                          const("idft_h", KX)[:, H * s:H * s + H], start=True, stop=True)
                    m.then_inc(idfth_mm, 1)
                for half in range(2):
                    pe.wait_ge(idfth_copy, START + 2 * b + half + 1)
                    if half == 0:
                        pe.wait_ge(out_mul, START + 8 * b)
                    else:
                        pe.wait_ge(out_mul, START + 8 * b + 4)
                    for c in range(16 * half, 16 * half + 16):
                        rows, at = slice(2 * C * (c % 2), 2 * C * (c % 2) + 2 * C), W * (c % 16 // 4)
                        m = pe.matmul(ps[:, 4 + c % 4, at:at + W], u[rows, c // 2, :], idftw[rows, :], start=True, stop=True)
                    m.then_inc(idftw_mm, 1)

        @block.scalar
        def _(act):
            def rows_of(image, b, chunk):
                return image[bass.ds(b, 1)].rearrange("a c (g r) w -> g (a c) (r w)", g=G)[:, :, chunk * NPX:chunk * NPX + NPX]

            act.wait_ge(par_loaded, 16 * PARS)
            act.wait_ge(init_done, 1)

            with act.Fori(0, B) as b:
                for chunk in range(CHUNKS):
                    par = chunk % 2
                    act.wait_ge(conv0_mm, START + b * CHUNKS + chunk + 1)
                    act.wait_ge(y_stored[par], START + 16 * (b * HALF + chunk // 2))
                    act.wait_ge(conv0_stat, START + b * CHUNKS + chunk)
                    nc.scalar.activation(lo[:, par, :], ps[:, SUM + par, :], ACT.Identity, bias=bias[:, 0:1]).then_inc(conv0_evac, 1)
                    act.wait_ge(conv0_evac, START + EVAC_CREDIT + b * CHUNKS + chunk + 1)
                    act.dma_start(rows_of(y_dram, b, chunk), lo[:, par, :]).then_inc(y_stored[par], 16)

            def group_root(gn, n):
                act.wait_ge(gn.shifted, START + n + 1)
                nc.scalar.activation(rstd[:, :], sd[:, :], ACT.Sqrt).then_inc(gn.root, 1)

            def relu(h, q):
                act.wait_ge(bn_applied, START + 4 * h + q + 1)
                c0 = QC * q
                nc.scalar.activation(yp[:, c0:c0 + QC, 4:YPW], tmp[:, c0:c0 + QC, :], ACT.Relu)
                nc.scalar.activation(yp[:, c0:c0 + QC, 0:4], tmp[:, c0:c0 + QC, W - 4:W], ACT.Relu).then_inc(relu_done, 1)

            def gradient(h, n):
                act.wait_ge(c3_mm, START + 8 * h + n + 1)
                act.wait_ge(c3_used, START + 8 * h + n)
                nc.scalar.activation(sq[:, :], ps[:, SIDE + 1, :], ACT.Square).then_inc(c3_sq, 1)

            def squares(h, q):
                act.wait_ge(gn1.out, START + h + 1)
                nc.scalar.activation(tmp[:, QC * q:QC * q + QC, :], xn[:, QC * q:QC * q + QC, 1:W + 1], ACT.Square).then_inc(norm_sq, 1)

            def head_steps(h, c):
                if 0 <= c - RELU_SLOT < 4:
                    relu(h, c - RELU_SLOT)
                n, part = divmod(c - FILT_SLOT - FILT_STEP, FILT_STEP)
                if 0 <= n < 8 and part == 0:
                    gradient(h, n)
                if c == NORM1_SLOT + 4:
                    group_root(gn1, h)
                if 0 <= c - NORM1_SLOT - 9 < 4:
                    squares(h, c - NORM1_SLOT - 9)
                if c == CHAN_SLOT + 3:
                    act.wait_ge(norm_sum, START + 4 * (h + 1))
                    nc.scalar.activation(rn[:, :], r2[:, :], ACT.Sqrt).then_inc(norm_root, 1)

            def conv3_out(t, chunk):
                act.wait_ge(conv3_mm, START + t * CHUNKS + chunk + 1)
                act.wait_ge(l3_stored, START + 16 * (t * CHUNKS + chunk))
                nc.scalar.activation(lo3[:, :], ps[:, SIDE + 1, :], ACT.Identity, bias=bias[:, 2:3]).then_inc(conv3_evac, 1)
                act.wait_ge(conv3_evac, START + t * CHUNKS + chunk + 1)
                act.dma_start(rows_of(l3_dram, t, chunk), lo3[:, :]).then_inc(l3_stored, 16)

            def tail_steps(t, c):
                if c == NORM2_SLOT + 7:
                    group_root(gn2, t)
                if c == NORM3_SLOT + 7:
                    group_root(gn3, t)
                if c == GRAY_SLOT + 6:
                    act.wait_ge(dog_mm, START + t + 1)
                    nc.scalar.copy(dog[:, 1:W + 1], ps[:, SIDE + 1, 0:W]).then_inc(dog_copy, 1)
                if c == GRAY_SLOT + 8:
                    act.wait_ge(sob_mm, START + t + 1)
                    nc.scalar.activation(r2[:, :], ps[:, SIDE, 0:W], ACT.Square)
                    nc.scalar.activation(rn[:, :], ps[:, SIDE + 1, 0:W], ACT.Square).then_inc(sob_sq, 1)
                if c == GRAY_SLOT + 9:
                    act.wait_ge(mag_sum, START + t + 1)
                    nc.scalar.activation(rn[:, :], ra[:, :], ACT.Sqrt).then_inc(mag_root, 1)
                    act.wait_ge(mag_root, START + t + 1)
                    nc.scalar.activation(r2[:, :], rn[:, :], ACT.Tanh, scale=gate_h[:, 0:1], bias=gate_h[:, 1:2]).then_inc(att_tanh, 1)
                if c > DFT_SLOT and (c - DFT_SLOT) % 2 == 1 and (c - DFT_SLOT) // 2 < 4:
                    n = (c - DFT_SLOT) // 2
                    act.wait_ge(dfth_mm, START + 4 * t + n + 1)
                    nc.scalar.copy(z[:, QC * n:QC * n + QC, :, :].rearrange("p c r x -> p (c r x)"), ps[:, SIDE, :]).then_inc(dfth_copy, 1)
                if c == RELU_SLOT:
                    act.wait_ge(dftw_mm, START + t + 1)
                    spectrum = ps[:, SIDE, 0:8 * 2 * MODES].rearrange("p (x r y) -> p r x y", x=8, r=2)
                    for n, (r, sign) in enumerate(((1, -1.0), (0, 1.0), (1, 1.0))):
                        nc.scalar.activation(cs[:, n, :, :, :, bass.ds(t, 1)].rearrange("p t x y b -> p (t x) (y b)"),
                                             spectrum[:, r, :, :], ACT.Copy, scale=sign).then_inc(dftw_copy, 1)
                n, part = divmod(c - FILT_SLOT, FILT_STEP)
                if 0 <= n < CHUNKS and part == 4:
                    conv3_out(t, n)

            def layer1(b, tail, head):
                def sum_out(b, chunk):
                    par = chunk % 2
                    act.wait_ge(mix_mm, START + MIX_CREDIT + b * SLOTS + (chunk + 1) * COMBOS)
                    act.wait_ge(l1_stored[par], START + 16 * (b * HALF + chunk // 2))
                    nc.scalar.activation(lo[:, par, :], ps[:, SUM + par, :], ACT.Identity, bias=bias[:, 1:2]).then_inc(sum_evac, 1)
                    act.wait_ge(sum_evac, START + EVAC_CREDIT + b * CHUNKS + chunk + 1)
                    act.dma_start(rows_of(l1_dram, b, chunk), lo[:, par, :]).then_inc(l1_stored[par], 16)

                for c in range(SLOTS):
                    for half in range(2):
                        n = 2 * c + half
                        act.wait_ge(spread_mm, START + b * BATCH_ITEMS + n + 1)
                        act.wait_ge(mix_mm, START + b * SLOTS + c)
                        nc.scalar.activation(ring[:, n % TRING, :], ps[:, 2 * half:2 * half + 2, :].rearrange("p a n -> p (a n)"),
                                             ACT.Tanh).then_inc(tanh_done, 1)
                    chunk, s = divmod(c, COMBOS)
                    if s == 3 and chunk:
                        sum_out(b, chunk - 1)
                    elif s == 3 and tail:
                        sum_out(b - 1, CHUNKS - 1)
                    if tail:
                        tail_steps(b - 1, c)
                    if head:
                        head_steps(b + 1, c)
                if not head:
                    sum_out(b, CHUNKS - 1)

            for c in range(SLOTS):
                head_steps(0, c)
            layer1(0, False, True)
            with act.Fori(1, B - 1) as b:
                layer1(b, True, True)
            layer1(B - 1, True, False)
            for c in range(SLOTS):
                tail_steps(B - 1, c)

            act.wait_ge(spec_mm, 1)
            for n in range(8):
                src = ps[:, n // 2, 256 * (n % 2):256 * (n % 2) + 256].rearrange("p (y r b) -> p b r y", y=MODES, r=2)
                nc.scalar.copy(ys[:, n, :, :].rearrange("p b (r y) -> p b r y", r=2), src).then_inc(spec_copy, 1)

            act.wait_ge(spec_loaded, 16)
            act.wait_ge(spec_copy, 8)
            with act.Fori(0, B) as b:
                act.wait_ge(idfth_mm, START + 2 * b)
                nc.scalar.copy(v2b, v2[:, :, bass.ds(b, 1), :].rearrange("p o b m -> p (o b) m")).then_inc(slice_done, 1)
                for half in range(2):
                    act.wait_ge(idfth_mm, START + 2 * b + half + 1)
                    act.wait_ge(idftw_mm, START + 2 * b)
                    for n in range(2):
                        m = nc.scalar.copy(u[:, 8 * half + 4 * n:8 * half + 4 * n + 4, :].rearrange("p a n -> p (a n)"), ps[:, 2 * half + n, :])
                    m.then_inc(idfth_copy, 1)

        def product(eng, b, n):
            chunk, s, half = n // ITEMS, n % ITEMS // 2, n % 2
            par = chunk % 2
            eng.wait_ge(tanh_done, START + TANH_CREDIT + b * BATCH_ITEMS + n + 1)
            eng.wait_ge(stack_loaded[par], START + LOAD_STACK * (b * HALF + chunk // 2 + 1))
            pixels = stack[:, par, stack_of(s), 2 * half:2 * half + 2, :].rearrange("p g (r w) -> p (g r) w", w=PW)[:, :, 0:W]
            slot = ring[:, n % TRING, :].rearrange("p (r w) -> p r w", w=W)
            return eng.tensor_tensor(slot, slot, pixels, ALU.mult)

        @block.gpsimd
        def _(pool):
            for s in counted:
                pool.sem_inc(s, START)
            for s, credit in ((conv0_evac, EVAC_CREDIT), (conv0_stat, EVAC_CREDIT), (sum_evac, EVAC_CREDIT),
                              (tanh_done, TANH_CREDIT), (mix_mm, MIX_CREDIT)):
                pool.sem_inc(s, credit)
            nc.gpsimd.memset(powers[:, :], -0.5)
            nc.gpsimd.memset(bsm[:, 6:7], 0.0).then_inc(init_done, 1)
            pool.wait_ge(init_done, 1)

            def group_root(gn, n):
                pool.wait_ge(gn.shifted, START + n + 1)
                nc.gpsimd.tensor_tensor(rstd[:, :], sd[:, :], powers[:, :], ALU.pow).then_inc(gn.root, 1)

            def pass1(b, last):
                if not last:
                    group_root(gn0, b + 1)

            group_root(gn0, 0)
            with pool.Fori(0, B - 1) as b:
                pass1(b, False)
            pool.wait_ge(bn_var, 1)
            nc.gpsimd.tensor_tensor(rstd[:, :], sd[:, :], powers[:, :], ALU.pow).then_inc(bn_sd, 1)

            with pool.Fori(0, B) as b:
                for n in range(BATCH_ITEMS):
                    if pool_item(n):
                        product(nc.gpsimd, b, n).then_inc(prod_pool, 1)

        @block.vector
        def _(dve):
            def quarter(tile, q):
                return tile[:, QC * q:QC * q + QC, :]

            def group_stats(gn, q):
                for c in range(QC * q, QC * q + QC):
                    m = nc.vector.bn_stats(st[:, c, :], xh[:, c, :])
                if q == 3:
                    m.then_inc(gn.stats, 1)

            def group_deviations(gn, n, t):
                dve.wait_ge(gn.mean, START + n + 1)
                t.inc(nc.vector.tensor_copy(mu[:, :], ps[:, SIDE, 0:C]))
                t.wait()
                for e, at in enumerate((1, 4)):
                    t.inc(nc.vector.tensor_tensor(dev2[:, :, e], st[:, :, at], mu[:, :], ALU.subtract))
                t.wait()
                t.inc(nc.vector.tensor_tensor(dev2[:, :, :], dev2[:, :, :], dev2[:, :, :], ALU.mult))
                t.wait()
                for e, at in enumerate((2, 5)):
                    m = nc.vector.scalar_tensor_tensor(out=dev[:, :, e], in0=dev2[:, :, e], scalar=float(W // 2), in1=st[:, :, at],
                                                       op0=ALU.mult, op1=ALU.add)
                m.then_inc(gn.dev, 1)

            GN_TICKS = 4

            def group_shift(gn, n):
                dve.wait_ge(gn.var, START + n + 1)
                nc.vector.tensor_scalar(sd[:, :], ps[:, SIDE, 0:C], GN_EPS, None, ALU.add).then_inc(gn.shifted, 1)

            def normalise(gn, n, q, t=None):
                if q == 0:
                    dve.wait_ge(gn.root, START + n + 1)
                    if t is not None:
                        t.inc(nc.vector.reciprocal(rstd[:, :], rstd[:, :]))
                        t.wait()
                for c in range(QC * q, QC * q + QC):
                    m = nc.vector.tensor_scalar(xn[:, c, 1:W + 1], xh[:, c, :], mu[:, c:c + 1], rstd[:, c:c + 1], ALU.subtract, ALU.mult)
                return m

            nc.vector.memset(tmp[:, 0, :], 0.0)
            nc.vector.memset(rp[:, :, :], 0.0).then_inc(zero_ready, 1)
            nc.vector.memset(xn[:, :, :], 0.0)
            nc.vector.memset(norms[:, :, :, :], 1.0)
            nc.vector.memset(gray[:, :], 0.0)
            nc.vector.memset(dog[:, :], 0.0)
            t = Ticks(dve, step0)
            t.inc(nc.vector.memset(opw[:, :, :], 0.0))
            t.wait()
            dve.wait_ge(const_loaded, 32)
            dve.wait_ge(par_loaded, 16 * PARS)
            nc.vector.tensor_scalar(gate_h[:, :], gate[:, :], 0.5, None, ALU.mult)
            parts = const("parts", KROWS)
            opf = opw[0:KROWS, :, :].rearrange("p s n -> p (s n)")
            t.inc(nc.vector.tensor_copy(opf, op_in))
            t.wait()
            t.inc(nc.vector.tensor_tensor(op_in, op_in, opf, ALU.subtract))
            t.wait()
            t.inc(nc.vector.tensor_scalar(op_rest, opf, parts[:, 0:1], None, ALU.mult))
            t.wait()
            t.inc(nc.vector.tensor_copy(opf, op_in))
            t.wait()
            t.inc(nc.vector.tensor_tensor(op_in, op_in, opf, ALU.subtract))
            t.inc(nc.vector.scalar_tensor_tensor(out=op_rest, in0=opf, scalar=parts[:, 1:2], in1=op_rest, op0=ALU.mult, op1=ALU.add))
            t.wait()
            t.inc(nc.vector.scalar_tensor_tensor(out=opf, in0=op_in, scalar=parts[:, 2:3], in1=op_rest, op0=ALU.mult, op1=ALU.add))
            t.wait()
            nc.vector.memset(bsm[:, 1:2], 0.0).then_inc(op_ready, 1)

            t.inc(nc.vector.tensor_tensor(f3[:, :], fil[:, 0:TAPS], fil[:, TAPS:], ALU.subtract))
            t.inc(nc.vector.memset(f5[:, :, :], 0.0))
            t.wait()
            t.inc(nc.vector.memset(f5[:, 0, 0:1], 1.0))
            t.wait()
            for f in range(2):
                fv = fil[:, TAPS * f:TAPS * f + TAPS].rearrange("p (a b) -> p a b", a=3)
                for a in range(3):
                    for c in range(3):
                        t.inc(nc.vector.scalar_tensor_tensor(out=f5[:, a:a + 3, c:c + 3], in0=fv, scalar=fv[:, a, c:c + 1],
                                                             in1=f5[:, a:a + 3, c:c + 3], op0=ALU.mult, op1=ALU.add))
                        t.wait()
            for d in range(8):
                for a in range(5 if d < 5 else 3):
                    s = f5[:, a, d:d + 1] if d < 5 else f3[:, 3 * a + d - 5:3 * a + d - 4]
                    if a == 0:
                        t.inc(nc.vector.tensor_scalar(circ[:, d, :], shift[:, a, :], s, None, ALU.mult))
                    else:
                        t.inc(nc.vector.scalar_tensor_tensor(out=circ[:, d, :], in0=shift[:, a, :], scalar=s, in1=circ[:, d, :],
                                                             op0=ALU.mult, op1=ALU.add))
                    t.wait()
            nc.vector.memset(ra[:, :], 0.0).then_inc(filt_ready, 1)
            n0 = t.n

            def pass1_norm(b, chunk, t):
                if chunk < 4:
                    if chunk == 0:
                        dve.wait_ge(x_loaded, START + 32 * (b + 1))
                    group_stats(gn0, chunk)
                if chunk == 4:
                    group_deviations(gn0, b, t)
                    group_shift(gn0, b)
                if chunk == 5:
                    dve.wait_ge(xn0_stored, START + 16 * b)
                    for q in range(4):
                        m = normalise(gn0, b, q)
                    m.then_inc(gn0.out, 1)

            def pass1(b, last):
                t = Ticks(dve, step0, n0 + GN_TICKS * (b + 1))
                for chunk in range(CHUNKS):
                    if not last:
                        pass1_norm(b + 1, chunk, t)
                    dve.wait_ge(conv0_evac, START + EVAC_CREDIT + b * CHUNKS + chunk + 1)
                    nc.vector.bn_stats(bst[:, bass.ds(b * CHUNKS + chunk, 1), :].rearrange("p a s -> p (a s)"),
                                       lo[:, chunk % 2, :]).then_inc(conv0_stat, 1)

            t = Ticks(dve, step0, n0)
            for chunk in range(CHUNKS):
                pass1_norm(0, chunk, t)
            with dve.Fori(0, B - 1) as b:
                pass1(b, False)
            pass1(B - 1, True)
            n0 += GN_TICKS * B

            t = Ticks(dve, step0, n0)
            dve.wait_ge(conv0_stat, START + EVAC_CREDIT + B * CHUNKS)
            nc.vector.bn_aggr(bagg[:, :], bst[:, :, :].rearrange("p a s -> p (a s)")).then_inc(bn_dev, 1)
            dve.wait_ge(bn_mat, 1)
            t.inc(nc.vector.tensor_copy(bsm[:, 2:3], ps[:, 0, 0:1]))
            t.wait()
            dve.wait_ge(bn_dev, 1)
            t.inc(nc.vector.tensor_tensor(bsm[:, 3:4], bagg[:, 0:1], bsm[:, 2:3], ALU.subtract))
            t.wait()
            t.inc(nc.vector.tensor_tensor(bsm[:, 4:5], bsm[:, 3:4], bsm[:, 3:4], ALU.mult))
            t.wait()
            t.inc(nc.vector.tensor_tensor(bsm[:, 5:6], bsm[:, 4:5], bagg[:, 1:2], ALU.add))
            t.wait()
            nc.vector.tensor_scalar(bexp[:, 0:C], const("eye_o"), bsm[:, 2:3], None, ALU.mult)
            nc.vector.tensor_scalar(bexp[:, C:2 * C], const("eye_o"), bsm[:, 5:6], None, ALU.mult).then_inc(bn_dev, 1)
            dve.wait_ge(bn_mat, 2)
            t.inc(nc.vector.tensor_copy(bn_m[:, :], ps[:, 1, 0:2 * C]))
            nc.vector.tensor_scalar(sd[:, :], ps[:, 1, C:2 * C], BN_EPS, None, ALU.add).then_inc(bn_var, 1)
            dve.wait_ge(bn_sd, 1)
            t.inc(nc.vector.tensor_tensor(bn_a[:, :], rstd[:, :], gam[:, 0:C], ALU.mult))
            t.wait()
            t.inc(nc.vector.tensor_tensor(bn_b[:, :], bn_m[:, 0:C], bn_a[:, :], ALU.mult))
            t.wait()
            t.inc(nc.vector.tensor_tensor(bn_b[:, :], gam[:, C:2 * C], bn_b[:, :], ALU.subtract))
            t.wait()
            for col in (0, PW - 1):
                m = nc.vector.memset(xn[:, :, col:col + 1], 0.0)
            m.then_inc(bn_ready, 1)

            HEAD_TICKS, TAIL_TICKS = GN_TICKS + 5, 2 * GN_TICKS + 3

            def head_steps(h, c, t, first=False):
                if 0 <= c - BN_SLOT < 4:
                    q = c - BN_SLOT
                    if q == 0:
                        dve.wait_ge(y_loaded, START + 32 * (h + 1))
                    for ch in range(QC * q, QC * q + QC):
                        m = nc.vector.tensor_scalar(tmp[:, ch, :], tmp[:, ch, :], bn_a[:, ch:ch + 1], bn_b[:, ch:ch + 1], ALU.mult, ALU.add)
                    m.then_inc(bn_applied, 1)
                n, part = divmod(c - FILT_SLOT, FILT_STEP)
                if 0 <= n < 8 and part == 5:
                    if n == 0:
                        dve.wait_ge(xh_loaded, START + 32 * (h + 1))
                    dve.wait_ge(c5_mm, START + 8 * h + n + 1)
                    xs = xh[:, 4 * n:4 * n + 4, :].rearrange("p c w -> p (c w)")
                    nc.vector.tensor_tensor(xs, xs, ps[:, SIDE, :], ALU.add).then_inc(c5_used, 1)
                n, part = divmod(c - FILT_SLOT - FILT_STEP, FILT_STEP)
                if 0 <= n < 8 and part == 0:
                    dve.wait_ge(c3_sq, START + 8 * h + n + 1)
                    dve.wait_ge(c5_used, START + 8 * h + n + 1)
                    xs = xh[:, 4 * n:4 * n + 4, :].rearrange("p c w -> p (c w)")
                    nc.vector.tensor_tensor(xs, xs, sq[:, :], ALU.add).then_inc(c3_used, 1)
                if 0 <= n < 8 and n % 2 == 1 and part == 1:
                    dve.wait_ge(c3_used, START + 8 * h + n + 1)
                    group_stats(gn1, n // 2)
                if c == NORM1_SLOT + 2:
                    group_deviations(gn1, h, t)
                if c == NORM1_SLOT + 3:
                    group_shift(gn1, h)
                if 0 <= c - NORM1_SLOT - 4 < 4:
                    q = c - NORM1_SLOT - 4
                    if q == 0 and not first:
                        dve.wait_ge(xn3_stored, START + 48 * (h - 1))
                        dve.wait_ge(dfth_mm, START + 4 * (h - 1))
                    m = normalise(gn1, h, q, t)
                    if q == 3:
                        t.inc(m)
                        t.wait()
                        for col in (0, PW - 1):
                            m = nc.vector.memset(xn[:, :, col:col + 1], 0.0)
                        m.then_inc(gn1.out, 1)
                if c == CHAN_SLOT + 2:
                    dve.wait_ge(norm_sq, START + 4 * (h + 1))
                    for q in range(4):
                        nc.vector.tensor_reduce(r2[:, 32 * q:32 * q + 32], tmp[:, :, 32 * q:32 * q + 32].rearrange("p c w -> p w c"),
                                                AX.X, ALU.add).then_inc(norm_sum, 1)
                if c == CHAN_SLOT + 3:
                    dve.wait_ge(norm_root, START + h + 1)
                    dve.wait_ge(parts_stored, START + 16 * h)
                    nc.vector.tensor_copy(rp[:, 0, 1:W + 1], rn[:, :]).then_inc(head_step, 1)
                    t.n += 1
                    t.wait()
                    t.inc(nc.vector.tensor_tensor(ra[:, :], rn[:, :], rp[:, 0, 1:W + 1], ALU.subtract))
                    t.wait()
                    t.inc(nc.vector.tensor_copy(rp[:, 1, 1:W + 1], ra[:, :]))
                    t.wait()
                    nc.vector.tensor_tensor(r2[:, :], ra[:, :], rp[:, 1, 1:W + 1], ALU.subtract).then_inc(norm_split_in, 1)
                    dve.wait_ge(norm_split_in, START + h + 1)
                    nc.vector.tensor_copy(rp[:, 2, 1:W + 1], r2[:, :]).then_inc(norm_split, 1)

            def tail_steps(t_, c, t, heads):
                if 0 <= c - X2_SLOT < 4:
                    q = c - X2_SLOT
                    if q == 0:
                        dve.wait_ge(x1_loaded, START + 32 * (t_ + 1))
                        dve.wait_ge(l1_loaded, START + 32 * (t_ + 1))
                    nc.vector.tensor_tensor(quarter(xh, q), quarter(xh, q), quarter(tmp, q), ALU.add).then_inc(x2_done, 1)
                if 0 <= c - NORM2_SLOT - 1 < 4:
                    q = c - NORM2_SLOT - 1
                    dve.wait_ge(x2_done, START + 4 * t_ + q + 1)
                    group_stats(gn2, q)
                if c == NORM2_SLOT + 5:
                    group_deviations(gn2, t_, t)
                if c == NORM2_SLOT + 6:
                    group_shift(gn2, t_)
                if 0 <= c - NORM2_SLOT - 8 < 4:
                    q = c - NORM2_SLOT - 8
                    if q == 0:
                        dve.wait_ge(xn1_stored, START + 16 * heads)
                        dve.wait_ge(norm_sq, START + 4 * heads)
                    m = normalise(gn2, t_, q, t)
                    if q == 3:
                        m.then_inc(gn2.out, 1)
                if 0 <= c - GRAY_SLOT < 4:
                    q = c - GRAY_SLOT
                    dve.wait_ge(gn2.out, START + t_ + 1)
                    nc.vector.tensor_reduce(gray[:, 2 + 32 * q:34 + 32 * q], xn[:, :, 1 + 32 * q:33 + 32 * q].rearrange("p c w -> p w c"),
                                            AX.X, ALU.add).then_inc(gray_done, 1)
                if c == GRAY_SLOT + 8:
                    dve.wait_ge(sob_sq, START + t_ + 1)
                    nc.vector.scalar_tensor_tensor(out=ra[:, :], in0=r2[:, :], scalar=MAG_EPS, in1=rn[:, :], op0=ALU.add, op1=ALU.add).then_inc(mag_sum, 1)
                if c == GRAY_SLOT + 10:
                    dve.wait_ge(att_tanh, START + t_ + 1)
                    nc.vector.tensor_scalar(ra[:, :], r2[:, :], 0.5, 1.5, ALU.mult, ALU.add).then_inc(gain_done, 1)
                if 0 <= c - ATT_SLOT < 4:
                    q = c - ATT_SLOT
                    dve.wait_ge(gain_done, START + t_ + 1)
                    gain = ra[:, :].rearrange("p (a w) -> p a w", a=1).to_broadcast([P, QC, W])
                    nc.vector.tensor_tensor(quarter(tmp, q), xn[:, QC * q:QC * q + QC, 1:W + 1], gain, ALU.mult).then_inc(att_mul, 1)
                if 0 <= c - ATT_SLOT - 4 < 4:
                    q = c - ATT_SLOT - 4
                    dve.wait_ge(att_mul, START + 4 * t_ + q + 1)
                    nc.vector.tensor_tensor(quarter(xh, q), quarter(xh, q), quarter(tmp, q), ALU.add).then_inc(x3_done, 1)
                if 0 <= c - NORM3_SLOT - 1 < 4:
                    q = c - NORM3_SLOT - 1
                    dve.wait_ge(x3_done, START + 4 * t_ + q + 1)
                    group_stats(gn3, q)
                if c == NORM3_SLOT + 5:
                    group_deviations(gn3, t_, t)
                if c == NORM3_SLOT + 6:
                    group_shift(gn3, t_)
                if 0 <= c - NORM3_SLOT - 8 < 4:
                    q = c - NORM3_SLOT - 8
                    m = normalise(gn3, t_, q, t)
                    if q == 3:
                        t.inc(m)
                        t.wait()
                        nc.vector.tensor_copy(xn[:, :, 0:1], xn[:, :, W:W + 1])
                        nc.vector.tensor_copy(xn[:, :, PW - 1:PW], xn[:, :, 1:2]).then_inc(gn3.out, 1)

            def layer1(b, tail, head):
                th = Ticks(dve, head_step, HEAD_TICKS * (b + 1))
                tt = Ticks(dve, tail_step, TAIL_TICKS * (b - 1)) if tail else None
                for c in range(SLOTS):
                    for n in (2 * c, 2 * c + 1):
                        if not pool_item(n):
                            product(nc.vector, b, n).then_inc(prod_dve, 1)
                    if tail:
                        tail_steps(b - 1, c, tt, b + 1)
                    if head:
                        head_steps(b + 1, c, th)
                assert not head or th.n == HEAD_TICKS, th.n
                assert not tail or tt.n == TAIL_TICKS, tt.n

            th = Ticks(dve, head_step)
            for c in range(SLOTS):
                head_steps(0, c, th, True)
            layer1(0, False, True)
            with dve.Fori(1, B - 1) as b:
                layer1(b, True, True)
            layer1(B - 1, True, False)
            tt = Ticks(dve, tail_step, TAIL_TICKS * (B - 1))
            for c in range(SLOTS):
                tail_steps(B - 1, c, tt, B)

            with dve.Fori(0, B // 2) as i:
                for par, (xt, lt) in enumerate(((xh, tmp), (xh2, tmp2))):
                    b = 2 * i + par
                    dve.wait_ge(x3_loaded[par], START + 32 * (i + 1))
                    dve.wait_ge(l3_loaded[par], START + 32 * (i + 1))
                    for half in range(2):
                        dve.wait_ge(idftw_mm, START + 2 * b + half + 1)
                        for q in range(4):
                            def pick(tile):
                                return tile[:, 16 * half:16 * half + 16, :].rearrange("p (n q) w -> p n q w", q=4)[:, :, q, :]
                            g = ps[:, 4 + q, :].rearrange("p (n w) -> p n w", n=4)
                            nc.vector.tensor_tensor(pick(lt), pick(lt), g, ALU.mult).then_inc(out_mul, 1)
                            dve.wait_ge(out_mul, START + 8 * b + 4 * half + q + 1)
                            nc.vector.tensor_tensor(pick(xt), pick(xt), pick(lt), ALU.add).then_inc(out_done, 1)


def _by_column(w_oikk):
    import numpy as np
    return np.transpose(w_oikk, (3, 1, 2, 0)).reshape(3 * C, 3, C)


def _stacked(w_oikk):
    import numpy as np
    w = np.transpose(w_oikk.reshape(C, C, TAPS), (2, 1, 0))
    r = np.zeros((4, C, STACKS, C), w.dtype)
    for j in range(TAPS):
        r[j % 4, :, j // 4, :] = w[j]
    return r.reshape(P, STACKS, C)


def _constants():
    import numpy as np
    k = np.zeros((P, NCONST + 5 * P), np.float64)

    def put(name, a):
        lo, hi = CONST[name]
        k[:a.shape[0], lo:hi] = a

    h = np.arange(P)
    put("mean", np.full((P, P), 1.0 / (2 * H)))
    put("var", np.full((P, P), 1.0 / (H * W)))
    put("same_o", (h[:, None] % C == h[None, :] % C) / G)
    put("quarter", np.full((P, P), 1.0 / G))
    put("eye_o", (h[:, None] % C == np.arange(C)[None, :]) * 1.0)
    k[:, NCONST:] = np.concatenate([h[:, None] == (h[None, :] - a) % H for a in range(5)], 1) * 1.0
    ax = np.arange(5) - 2.0
    g = [np.exp(-(ax[:, None] ** 2 + ax[None, :] ** 2) / (2.0 * s * s)) for s in (1.0, 2.0)]
    k5 = (g[0] / g[0].sum() - g[1] / g[1].sum()) / C
    band = lambda col, r: sum(col[d] * (h[:, None] == h[None, :] + d - r) for d in range(len(col)))
    put("dog", np.concatenate([band(k5[:, d], 2) for d in range(5)], 1))
    sob = [(-1, -2, -1), (1, 2, 1), (-1, 0, 1), (-2, 0, 2), (-1, 0, 1)]
    put("sobel", np.concatenate([band(c, 1) for c in sob], 1))
    kx = np.concatenate([np.arange(MODES), np.arange(H - MODES, H)])
    th = 2 * np.pi * np.outer(h, kx) / H
    put("dft_h", np.concatenate([np.cos(th), -np.sin(th)], 1))
    ky = np.arange(MODES)
    tw = 2 * np.pi * np.outer(h, ky) / W
    put("dft_w", np.concatenate([np.cos(tw), -np.sin(tw), np.sin(tw), np.cos(tw)], 1))
    put("idft_h", np.concatenate([np.cos(th.T), np.sin(th.T)], 1))
    a = (np.where(ky == 0, 1.0, 2.0) / (H * W))[:, None]
    cw, sw = a * np.cos(tw.T), a * np.sin(tw.T)
    put("idft_w", np.tile(np.concatenate([cw, -sw, -sw, -cw], 0), (2, 1)))
    put("parts", np.array([[float(p == r) for p in range(3)] for r in range(BIAS_ROWS)]
                          + [[float(p == wp) for p in range(3)] for wp, _ in PAIRS for _ in range(TAPS)]))
    return k.astype(np.float32)


def kernel(**inputs):
    import numpy as np
    import concourse.bacc as _bacc
    from concourse.bass_utils import run_bass_kernel_spmd as _run

    v = {n: np.asarray(a) for n, a in inputs.items()}
    op_w, op_b = v["L1_conv_op_w"], v["L1_conv_op_b"]
    w1 = v["L1_conv_weight"].reshape(C, C, TAPS)
    op_rows = np.zeros((KROWS, COMBOS, 4, C), np.float32)
    mix = np.zeros((4, C, COMBOS, C), np.float32)
    for s in range(COMBOS):
        for q in range(4):
            if tap_pair(s, q) is None:
                continue
            j, kk = tap_pair(s, q)
            op_rows[:BIAS_ROWS, s, q, :] = op_b[TAPS * j + kk]
            for n in range(len(PAIRS)):
                op_rows[BIAS_ROWS + TAPS * n:BIAS_ROWS + TAPS * n + TAPS, s, q, :] = op_w[TAPS * j + kk][:, None]
            mix[q, :, s, :] = w1[:, :, kk]
    tile4 = lambda a: np.tile(a.reshape(C, 1), (G, 1))
    arrays = {
        "x": v["x"], "conv0_w": _by_column(v["L0_conv_conv_w"]), "conv0_b": tile4(v["L0_conv_conv_b"]),
        "bn_gamma": v["L0_conv_bn_gamma"], "bn_beta": v["L0_conv_bn_beta"],
        "filt_x": v["L0_conv_filt_x"].reshape(TAPS), "filt_y": v["L0_conv_filt_y"].reshape(TAPS),
        "conv1_w": _stacked(np.transpose(v["L1_conv_weight"], (1, 0, 2, 3))), "mix1_w": mix.reshape(P, COMBOS, C),
        "conv1_b": tile4(v["L1_conv_bias"]), "op_rows": op_rows.reshape(KROWS, COMBOS * P),
        "gate_w": v["L2_conv_gate_w"], "gate_b": v["L2_conv_gate_b"],
        "w1r": v["L3_conv_w1r"], "w1i": v["L3_conv_w1i"], "w2r": v["L3_conv_w2r"], "w2i": v["L3_conv_w2i"],
        "conv3_w": _by_column(v["L3_conv_conv_w"]), "conv3_b": tile4(v["L3_conv_conv_b"]), "consts": _constants(),
    }
    nc = _bacc.Bacc("TRN2", target_bir_lowering=False, num_devices=1)
    given, args = {}, []
    for name, a in arrays.items():
        a = np.ascontiguousarray(a)
        given["in_" + name] = a
        args.append(nc.dram_tensor("in_" + name, a.shape, mybir.dt.from_np(a.dtype), kind="ExternalInput").ap())
    args.append(nc.dram_tensor("out_0", (B, C, H, W), F32, kind="ExternalOutput").ap())
    four_layers(nc, *args)
    r = _run(nc, [given], core_ids=[0])
    return r.results[0]["out_0"]
```
